# Optimizing a Trainium2 kernel written in Bass

```python
import numpy as np
import jax
import jax.numpy as jnp

def _softmax(x, axis=-1):
    return jax.nn.softmax(x, axis=axis)

def _gelu(x):
    return jax.nn.gelu(x, approximate=True)

def _silu(x):
    return jax.nn.silu(x)

def _sigmoid(x):
    return jax.nn.sigmoid(x)

def _layernorm(x, axis=-1, eps=1e-05):
    m = jnp.mean(x, axis=axis, keepdims=True)
    v = jnp.var(x, axis=axis, keepdims=True)
    return (x - m) / jnp.sqrt(v + eps)

def _scatter_add(tgt, idx, src, axis=0):
    return tgt.at[idx].add(src)

def _segment_sum(src, seg, n):
    return jax.ops.segment_sum(src, seg, n)
kernel_name = 'mk_audio_tower_d2_tok_audfeat256_r4_e47ce2'

def setup_inputs(seed: int=0):
    np.random.seed(seed)
    _w = jnp.asarray

    def _rec_inputs():
        import jax
        import jax.numpy as jnp
        _rk = jax.random.key(seed)
        x = -0.000392918 + 0.999932 * jax.random.normal(jax.random.fold_in(_rk, 1), (32, 512, 128), jnp.float32)
        return x
    x = _rec_inputs()

    def _L0_tok_setup():
        import jax, jax.numpy as jnp
        from jax import lax
        import numpy as np
        BN_EPS = 0.001

        @jax.custom_vjp
        def ste_sign(x):
            return jnp.where(x >= 0, 1.0, -1.0).astype(x.dtype)

        def _ste_fwd(x):
            return (ste_sign(x), x)

        def _ste_bwd(x, g):
            return (g * (jnp.abs(x) <= 1.0).astype(g.dtype),)
        ste_sign.defvjp(_ste_fwd, _ste_bwd)
        key = jax.random.key(seed)
        ks = jax.random.split(key, 6)
        x = jax.random.normal(ks[0], (64, 512, 128), dtype=jnp.float32)
        kernel = jax.random.normal(ks[1], (3, 128, 64), dtype=jnp.float32) * 0.05
        bias = jax.random.normal(ks[2], (64,), dtype=jnp.float32) * 0.01
        beta = jax.random.normal(ks[3], (64,), dtype=jnp.float32) * 0.01
        moving_mean = jax.random.normal(ks[4], (64,), dtype=jnp.float32) * 0.1
        moving_var = jax.random.uniform(ks[5], (64,), dtype=jnp.float32) + 0.5
        return {'x': x, 'kernel': kernel, 'bias': bias, 'beta': beta, 'moving_mean': moving_mean, 'moving_var': moving_var}
    _L0_tok_all = _L0_tok_setup()
    _L0_tok_in = {k: v for k, v in _L0_tok_all.items() if k in ('kernel', 'bias', 'beta', 'moving_mean', 'moving_var')}
    del _L0_tok_all

    def _L0_attn_setup():
        import jax, jax.numpy as jnp
        import numpy as np
        from math import sqrt
        DIM = 64
        key = jax.random.key(seed)
        k1, k2, k3, k4 = jax.random.split(key, 4)
        B, T, D, H, R = (2, 1024, DIM, 8, 32)

        def xavier(k, shape, fan_in, fan_out):
            a = sqrt(6.0 / (fan_in + fan_out))
            return jax.random.uniform(k, shape, jnp.float32, -a, a)
        x = jax.random.normal(k1, (B, T, D), jnp.float32)
        Q = xavier(k2, (H, R, D), D, R)
        K = xavier(k3, (H, R, D), D, R)
        VO = xavier(k4, (H, D, D), D, D)
        return {'x': x, 'Q': Q, 'K': K, 'VO': VO}
    _L0_attn_all = _L0_attn_setup()
    _L0_attn_in = {k: v for k, v in _L0_attn_all.items() if k in ('Q', 'K', 'VO')}
    del _L0_attn_all

    def _L0_ffn_setup():
        import jax, jax.numpy as jnp
        import numpy as np
        C = 64
        HID = 256
        E = 8
        TEMP = 1.0
        key = jax.random.key(seed)
        ks = jax.random.split(key, 7)
        x = jax.random.normal(ks[0], (8, 4096, C), dtype=jnp.float32)
        W1 = jax.random.normal(ks[1], (C, HID), dtype=jnp.float32) * 0.02
        b1 = jnp.zeros((HID,), dtype=jnp.float32)
        Wg = jax.random.normal(ks[2], (HID, E), dtype=jnp.float32) * 0.02
        bg = jnp.zeros((E,), dtype=jnp.float32)
        Wd = jax.random.normal(ks[3], (E, HID, C), dtype=jnp.float32) * 0.02
        bd = jnp.zeros((E, C), dtype=jnp.float32)
        return {'x': x, 'W1': W1, 'b1': b1, 'Wg': Wg, 'bg': bg, 'Wd': Wd, 'bd': bd}
    _L0_ffn_all = _L0_ffn_setup()
    _L0_ffn_in = {k: v for k, v in _L0_ffn_all.items() if k in ('W1', 'b1', 'Wg', 'bg', 'Wd', 'bd')}
    del _L0_ffn_all

    def _L1_attn_setup():
        import jax, jax.numpy as jnp
        import numpy as np
        B, L, D = (4, 1024, 64)
        key = jax.random.key(seed)
        kx, kq, kk, kv, ko = jax.random.split(key, 5)
        std = 0.02
        return {'x': jax.random.normal(kx, (B, L, D), dtype=jnp.float32), 'Wq': std * jax.random.normal(kq, (D, D), dtype=jnp.float32), 'Wk': std * jax.random.normal(kk, (D, D), dtype=jnp.float32), 'Wv': std * jax.random.normal(kv, (D, D), dtype=jnp.float32), 'Wo': std * jax.random.normal(ko, (D, D), dtype=jnp.float32)}
    _L1_attn_all = _L1_attn_setup()
    _L1_attn_in = {k: v for k, v in _L1_attn_all.items() if k in ('Wq', 'Wk', 'Wv', 'Wo')}
    del _L1_attn_all

    def _L1_ffn_setup():
        import jax, jax.numpy as jnp
        import numpy as np
        E, D, H, TOP_K = (6, 64, 64, 2)
        ROUTER_H = D // 2
        key = jax.random.key(seed)
        ks = jax.random.split(key, 12)
        s = 1.0 / np.sqrt(D)
        sh = 1.0 / np.sqrt(H)
        sr = 1.0 / np.sqrt(ROUTER_H)
        return {'features': jax.random.normal(ks[0], (8, 1024, D), dtype=jnp.float32), 'router_w1': jax.random.uniform(ks[1], (D, ROUTER_H), jnp.float32, -s, s), 'router_b1': jnp.zeros((ROUTER_H,), jnp.float32), 'router_w2': jax.random.uniform(ks[2], (ROUTER_H, E), jnp.float32, -sr, sr), 'router_b2': jnp.zeros((E,), jnp.float32), 'expert_w1': jax.random.uniform(ks[3], (E, D, H), jnp.float32, -s, s), 'expert_b1': jnp.zeros((E, H), jnp.float32), 'expert_w2': jax.random.uniform(ks[4], (E, H, H), jnp.float32, -sh, sh), 'expert_b2': jnp.zeros((E, H), jnp.float32), 'expert_w3': jax.random.uniform(ks[5], (E, H, D), jnp.float32, -sh, sh), 'expert_b3': jnp.zeros((E, D), jnp.float32)}
    _L1_ffn_all = _L1_ffn_setup()
    _L1_ffn_in = {k: v for k, v in _L1_ffn_all.items() if k in ('router_w1', 'router_b1', 'router_w2', 'router_b2', 'expert_w1', 'expert_b1', 'expert_w2', 'expert_b2', 'expert_w3', 'expert_b3')}
    del _L1_ffn_all
    return {'x': x, 'L0_tok_kernel': _L0_tok_in['kernel'], 'L0_tok_bias': _L0_tok_in['bias'], 'L0_tok_beta': _L0_tok_in['beta'], 'L0_tok_moving_mean': _L0_tok_in['moving_mean'], 'L0_tok_moving_var': _L0_tok_in['moving_var'], 'L0_attn_Q': _L0_attn_in['Q'], 'L0_attn_K': _L0_attn_in['K'], 'L0_attn_VO': _L0_attn_in['VO'], 'L0_ffn_W1': _L0_ffn_in['W1'], 'L0_ffn_b1': _L0_ffn_in['b1'], 'L0_ffn_Wg': _L0_ffn_in['Wg'], 'L0_ffn_bg': _L0_ffn_in['bg'], 'L0_ffn_Wd': _L0_ffn_in['Wd'], 'L0_ffn_bd': _L0_ffn_in['bd'], 'L1_attn_Wq': _L1_attn_in['Wq'], 'L1_attn_Wk': _L1_attn_in['Wk'], 'L1_attn_Wv': _L1_attn_in['Wv'], 'L1_attn_Wo': _L1_attn_in['Wo'], 'L1_ffn_router_w1': _L1_ffn_in['router_w1'], 'L1_ffn_router_b1': _L1_ffn_in['router_b1'], 'L1_ffn_router_w2': _L1_ffn_in['router_w2'], 'L1_ffn_router_b2': _L1_ffn_in['router_b2'], 'L1_ffn_expert_w1': _L1_ffn_in['expert_w1'], 'L1_ffn_expert_b1': _L1_ffn_in['expert_b1'], 'L1_ffn_expert_w2': _L1_ffn_in['expert_w2'], 'L1_ffn_expert_b2': _L1_ffn_in['expert_b2'], 'L1_ffn_expert_w3': _L1_ffn_in['expert_w3'], 'L1_ffn_expert_b3': _L1_ffn_in['expert_b3']}

def reference(x, L0_tok_kernel, L0_tok_bias, L0_tok_beta, L0_tok_moving_mean, L0_tok_moving_var, L0_attn_Q, L0_attn_K, L0_attn_VO, L0_ffn_W1, L0_ffn_b1, L0_ffn_Wg, L0_ffn_bg, L0_ffn_Wd, L0_ffn_bd, L1_attn_Wq, L1_attn_Wk, L1_attn_Wv, L1_attn_Wo, L1_ffn_router_w1, L1_ffn_router_b1, L1_ffn_router_w2, L1_ffn_router_b2, L1_ffn_expert_w1, L1_ffn_expert_b1, L1_ffn_expert_w2, L1_ffn_expert_b2, L1_ffn_expert_w3, L1_ffn_expert_b3):
    import jax
    import jax.numpy as jnp

    def _L0_tok_ref(x, kernel, bias, beta, moving_mean, moving_var):
        import jax, jax.numpy as jnp
        from jax import lax
        import numpy as np
        BN_EPS = 0.001

        @jax.custom_vjp
        def ste_sign(x):
            return jnp.where(x >= 0, 1.0, -1.0).astype(x.dtype)

        def _ste_fwd(x):
            return (ste_sign(x), x)

        def _ste_bwd(x, g):
            return (g * (jnp.abs(x) <= 1.0).astype(g.dtype),)
        ste_sign.defvjp(_ste_fwd, _ste_bwd)
        xq = ste_sign(x)
        kq = ste_sign(kernel)
        y = lax.conv_general_dilated(xq, kq, window_strides=(1,), padding='VALID', dimension_numbers=('NWC', 'WIO', 'NWC'))
        y = y + bias
        inv = lax.rsqrt(moving_var + BN_EPS)
        return (y - moving_mean) * inv + beta

    def _L0_attn_ref(x, Q, K, VO):
        import jax, jax.numpy as jnp
        import numpy as np
        from math import sqrt
        DIM = 64
        d = x.shape[-1]
        q = jnp.einsum('btd,hrd->bhtr', x, Q)
        k = jnp.einsum('bud,hrd->bhur', x, K)
        scores = jnp.einsum('bhtr,bhur->bhtu', q, k) / sqrt(d)
        attn = jax.nn.softmax(scores, axis=-1)
        ctx = jnp.einsum('bhtu,bud->bhtd', attn, x)
        out = jnp.einsum('bhtd,hde->bte', ctx, VO)
        return out

    def _L0_ffn_ref(x, W1, b1, Wg, bg, Wd, bd):
        import jax, jax.numpy as jnp
        import numpy as np
        C = 64
        HID = 256
        E = 8
        TEMP = 1.0
        orig_shape = x.shape
        xf = x.reshape(-1, orig_shape[-1])
        H = jax.nn.gelu(xf @ W1 + b1, approximate=False)
        probs = jax.nn.softmax((H @ Wg + bg) / TEMP, axis=-1)
        assign = jnp.argmax(probs, axis=-1)
        out = jnp.zeros_like(xf)
        for e in range(Wd.shape[0]):
            y = H @ Wd[e] + bd[e]
            sel = (assign == e)[:, None]
            out = out + jnp.where(sel, probs[:, e:e + 1] * y, 0.0)
        return out.reshape(orig_shape)

    def _L1_attn_ref(x, Wq, Wk, Wv, Wo):
        import jax, jax.numpy as jnp
        import numpy as np
        B, L, D = (4, 1024, 64)
        q = x @ Wq.T
        k = x @ Wk.T
        v = x @ Wv.T
        logits = jnp.einsum('bld,bmd->blm', q, k)
        Lq = x.shape[1]
        causal_mask = jnp.triu(jnp.ones((Lq, Lq), dtype=bool), k=1)
        logits = jnp.where(causal_mask[None], jnp.asarray(0.0, logits.dtype), logits)
        attn = jax.nn.relu(logits)
        row_counts = jnp.maximum(jnp.arange(Lq, dtype=attn.dtype), 1.0)
        attn = attn / row_counts[None, :, None]
        ctx = jnp.einsum('blm,bmd->bld', attn, v)
        return ctx @ Wo.T

    def _L1_ffn_ref(features, router_w1, router_b1, router_w2, router_b2, expert_w1, expert_b1, expert_w2, expert_b2, expert_w3, expert_b3):
        import jax, jax.numpy as jnp
        import numpy as np
        E, D, H, TOP_K = (6, 64, 64, 2)
        ROUTER_H = D // 2
        rh = jax.nn.relu(features @ router_w1 + router_b1)
        expert_logits = jax.nn.softmax(rh @ router_w2 + router_b2, axis=-1)
        top_w, top_i = jax.lax.top_k(expert_logits, TOP_K)
        routing_weights = jax.nn.softmax(top_w, axis=-1)
        h1 = jax.nn.relu(jnp.einsum('bsd,edh->bseh', features, expert_w1) + expert_b1)
        h2 = jax.nn.relu(jnp.einsum('bseh,ehf->bsef', h1, expert_w2) + expert_b2)
        expert_out = jnp.einsum('bsef,efo->bseo', h2, expert_w3) + expert_b3
        sel = jnp.take_along_axis(expert_out, top_i[:, :, :, None], axis=2)
        combined = jnp.sum(sel * routing_weights[..., None], axis=2)
        return combined
    h = _L0_tok_ref(x, L0_tok_kernel, L0_tok_bias, L0_tok_beta, L0_tok_moving_mean, L0_tok_moving_var)
    h = h + _L0_attn_ref(_layernorm(h, axis=-1), L0_attn_Q, L0_attn_K, L0_attn_VO)
    h = h + _L0_ffn_ref(_layernorm(h, axis=-1), L0_ffn_W1, L0_ffn_b1, L0_ffn_Wg, L0_ffn_bg, L0_ffn_Wd, L0_ffn_bd)
    h = h + _L1_attn_ref(_layernorm(h, axis=-1), L1_attn_Wq, L1_attn_Wk, L1_attn_Wv, L1_attn_Wo)
    h = h + _L1_ffn_ref(_layernorm(h, axis=-1), L1_ffn_router_w1, L1_ffn_router_b1, L1_ffn_router_w2, L1_ffn_router_b2, L1_ffn_expert_w1, L1_ffn_expert_b1, L1_ffn_expert_w2, L1_ffn_expert_b2, L1_ffn_expert_w3, L1_ffn_expert_b3)
    return h

_drawn_inputs = setup_inputs


def setup_inputs(seed=0):
    import zlib

    import numpy as np

    out = dict(_drawn_inputs(seed))
    spreads = {'L0_ffn_b1': (0.0, 0.8),
     'L0_ffn_bg': (0.0, 0.8),
     'L0_ffn_bd': (0.0, 0.8),
     'L1_ffn_router_b1': (0.0, 0.8),
     'L1_ffn_router_b2': (0.0, 0.8),
     'L1_ffn_expert_b1': (0.0, 0.8),
     'L1_ffn_expert_b2': (0.0, 0.8),
     'L1_ffn_expert_b3': (0.0, 2.0)}
    factors = {'L0_tok_bias': 8.0,
     'L0_tok_beta': 8.0,
     'L0_tok_moving_mean': 8.0,
     'L0_attn_Q': 2.762,
     'L0_attn_K': 2.688,
     'L0_ffn_W1': 8.0,
     'L0_ffn_Wg': 8.0,
     'L0_ffn_Wd': 8.0,
     'L1_attn_Wq': 8.0,
     'L1_attn_Wk': 8.0,
     'L1_attn_Wv': 8.0,
     'L1_attn_Wo': 8.0,
     'L1_ffn_router_w1': 8.0,
     'L1_ffn_router_w2': 8.0,
     'L1_ffn_expert_w1': 8.0,
     'L1_ffn_expert_w2': 8.0,
     'L1_ffn_expert_w3': 8.0}
    for name, (base, spread) in spreads.items():
        noise = np.random.default_rng([zlib.crc32(name.encode()), seed]).standard_normal(out[name].shape)
        drawn = base * np.exp(spread * noise) if base else spread * noise
        out[name] = jnp.asarray(drawn.astype(out[name].dtype))
    for name, factor in factors.items():
        out[name] = (out[name] * factor).astype(out[name].dtype)
    return out
```

```python
import concourse.bass as bass
import concourse.mybir as mybir
from contextlib import ExitStack

F32 = mybir.dt.float32
F16 = mybir.dt.float16
BF16 = mybir.dt.bfloat16
I32 = mybir.dt.int32
ALU = mybir.AluOpType
ACT = mybir.ActivationFunctionType
AX = mybir.AxisListType.X

P = 128
B, T_IN, C_IN = 32, 512, 128
TAPS, D = 3, 64
T = T_IN - TAPS + 1
NB = T_IN // P
H0, R0 = 8, 32
PAIRS = H0 // 2
HID, E0 = 256, 8
HB = HID // P
E1, RH = 6, 32
EP = E1 // 2
SLOTS = H0 * NB
TAIL = T - (NB - 1) * P

XS, WS = 64.0, 256.0
ZS = 1.0 / 128.0
LIN = XS * WS
LOGIT = LIN * ZS * XS
LN_EPS, BN_EPS = 1e-5, 1e-3
TINY = 1e-30

W_HID, W_Z, W_V, W_R, W_E = 0, HID, HID + D, HID + 2 * D, HID + 2 * D + RH
W_ALL = W_E + E1 * D
SEGMENTS = [(W_HID, W_Z), (W_Z, W_V), (W_V, W_R), (W_R, W_E), (W_E, W_ALL)]
SG_HID, SG_Z, SG_V, SG_R, SG_E = range(H0, H0 + 5)
N_SG = H0 + 5
R_D, R_3, R_G, R_L = 0, E0 * D, E0 * D + E1 * D, E0 * D + E1 * D + NB * E0
R_ALL = R_L + NB * E1

LAG = {"front": 0, "attn": 1, "mid": 2, "late": 3}
STEPS = B + max(LAG.values())

TURNS = [
    (1, "late", "xt3", 0), (1, "attn", "z", 1),
    (3, "late", "zl", 0),
    (4, "late", "vl", 0),
    (5, "attn", "z", 2), (5, "late", "lg", 0),
    (6, "late", "lg", 1),
    (7, "late", "lg", 2),
    (8, "mid", "vo", 0), (8, "late", "lg", 3),
    (9, "attn", "z", 3), (9, "mid", "vo", 1),
    (10, "mid", "vo", 2),
    (11, "mid", "vo", 3), (11, "front", "xq", 0),
    (12, "late", "av", 0),
    (13, "attn", "z", 4),
    (14, "front", "conv", 0),
    (16, "mid", "xt2", 0),
    (17, "attn", "z", 5),
    (18, "late", "xt4", 0), (18, "mid", "hid", 0),
    (19, "mid", "hid", 1),
    (20, "front", "xt1", 0), (20, "late", "rh", 0),
    (21, "attn", "z", 6), (21, "late", "e1", 0),
    (22, "mid", "gate", 0), (22, "late", "e1", 1),
    (23, "late", "rl", 0), (23, "late", "e1", 2),
    (24, "mid", "y", 0), (24, "late", "e2", 0),
    (25, "attn", "z", 7), (25, "mid", "y", 1),
    (26, "mid", "y", 2), (26, "late", "e2", 1),
    (27, "mid", "y", 3), (27, "late", "e2", 2),
    (28, "late", "o", 0),
    (29, "front", "z", 0), (29, "late", "o", 1),
    (30, "late", "o", 2),
    (31, "late", "o", 3),
]


def begun(b):
    return not isinstance(b, int) or b >= 0


class Signal:

    def __init__(self, sem, per, unit=1):
        self.sem, self.per, self.unit = sem, per, unit

    def at(self, b, k=0):
        return b * (self.per * self.unit) + (k + 1) * self.unit

    def before(self, b, k, back):
        k -= back
        while k < 0:
            b, k = b - 1, k + self.per
        return b, k


class Chain:

    def __init__(self, sem, per):
        self.sem, self.per, self.n = sem, per, 0

    def link(self, eng, b, ins):
        ins.then_inc(self.sem, 1)
        self.n += 1
        eng.wait_ge(self.sem, b * self.per + self.n)

    def end(self):
        assert self.n == self.per, (self.n, self.per)
        self.n = 0


def tower(nc, x, kern, bias, beta, mean, var, Q, K, VO, W1, b1, Wg, bg, Wd, bd, Wq, Wk, Wv, Wo,
          rw1, rb1, rw2, rb2, ew1, eb1, ew2, eb2, ew3, eb3, out):
    ctx = ExitStack()
    with ctx:
        def sb(name, shape, dt=F32):
            return ctx.enter_context(nc.sbuf_tensor(name, shape, dt))

        def ps(name):
            return ctx.enter_context(nc.psum_tensor(name, [P, 512], F32))

        def sem(name):
            return ctx.enter_context(nc.semaphore(name))

        def signal(name, per=1, unit=1):
            return Signal(sem(name), per, unit)

        q_dup = sb("q_dup", [R0, H0, 2, D])
        k_raw = sb("k_raw", [R0, H0, D])
        wq_dup = sb("wq_dup", [D, 2, D])
        wv_dup = sb("wv_dup", [D, 2, D])
        wk_raw = sb("wk_raw", [D, D])
        wo_raw = sb("wo_raw", [D, D])
        wo_t = sb("wo_t", [D, D])
        w_raw = sb("w_raw", [P, W_ALL])
        w_nrm = sb("w_nrm", [P, W_ALL])
        a_nrm = sb("a_nrm", [P, H0, D])
        w_hi = sb("w_hi", [P, W_ALL], F16)
        w_lo = sb("w_lo", [P, W_ALL], F16)
        a_w = sb("a_w", [P, H0, 2, 2, D], F16)
        z_w = sb("z_w", [P, 2, 2, D], F16)
        amax = sb("amax", [P, N_SG])
        sigma = sb("sigma", [P, N_SG])
        rsigma = sb("rsigma", [P, N_SG])
        exp_scale = sb("exp_scale", [P, H0])
        hid_scale = sb("hid_scale", [P, 1])
        unscale = sb("unscale", [P, N_SG])
        rescale = sb("rescale", [P, N_SG])
        vo_w = sb("vo_w", [P, PAIRS, P])
        wd_w = sb("wd_w", [P, HB, E0 * D])
        wg_w = sb("wg_w", [P, HB, E0])
        b1_c = sb("b1_c", [P, HB])
        rw2_w = sb("rw2_w", [RH, E1])
        rb1_c = sb("rb1_c", [RH, 1])
        e2_w = sb("e2_w", [P, EP, P])
        e3_w = sb("e3_w", [P, EP, P])
        eb1_c = sb("eb1_c", [P, EP])
        eb2_c = sb("eb2_c", [P, EP])
        row = sb("row", [1, R_ALL])
        row_rest = sb("row_rest", [1, 2, R_ALL])
        row_part = sb("row_part", [1, 3, R_ALL], BF16)
        bias_rows = sb("bias_rows", [3, R_ALL], BF16)
        ones_rows = sb("ones_rows", [3, P], BF16)
        k_raw0 = sb("k_raw0", [P, TAPS, D])
        k_sign = sb("k_sign", [P, TAPS, D], BF16)
        bn_raw = sb("bn_raw", [P, 4, D])
        bn_inv = sb("bn_inv", [P, D])
        bn_exp = sb("bn_exp", [P, D])
        bn_scale = sb("bn_scale", [P, D])
        bn_shift = sb("bn_shift", [P, D])
        id32 = sb("id32", [P, P])
        id16 = sb("id16", [P, P], F16)
        idb = sb("idb", [P, P], BF16)
        causal = sb("causal", [P, 512])
        row_no = sb("row_no", [P, NB], I32)
        row_scale = sb("row_scale", [P, NB])
        rank_i = sb("rank_i", [P, E0], I32)
        rank = sb("rank", [P, E0])
        minus_half = sb("minus_half", [P, NB])

        x_in = sb("x_in", [P, NB, C_IN])
        x_sign = sb("x_sign", [P, NB, C_IN], BF16)
        xq_t = sb("xq_t", [P, T_IN + TAPS - 1], BF16)
        h0 = [sb(f"h0_{i}", [P, NB, D]) for i in range(2)]
        ln = []
        for i in range(4):
            ln.append(dict(
                sum=sb(f"ln{i}_sum", [P, NB]), mu=sb(f"ln{i}_mu", [P, NB]),
                d=sb(f"ln{i}_d", [P, NB, D]), sq=sb(f"ln{i}_sq", [P, NB, D]),
                sum2=sb(f"ln{i}_sum2", [P, NB]), var=sb(f"ln{i}_var", [P, NB]),
                r=sb(f"ln{i}_r", [P, NB]), parts=sb(f"ln{i}_parts", [P, NB, 2 * D], F16)))
        xn1 = [sb(f"xn1_{i}", [P, NB, D]) for i in range(2)]
        xn_other = [sb(f"xn_{i}", [P, NB, D]) for i in (2, 3, 4)]
        xt1 = [sb(f"xt1_{i}", [P, 512], F16) for i in range(2)]
        xt2, xt3, xt4 = (sb(f"xt{i}", [P, 512], F16) for i in (2, 3, 4))
        z_t = [sb(f"z_t{i}", [P, 2, 512], F16) for i in range(2)]
        neg_max = sb("neg_max", [P, SLOTS])
        exp_bias = sb("exp_bias", [P, SLOTS])
        row_sum = [sb(f"row_sum{i}", [P, SLOTS]) for i in range(2)]
        probs = [sb(f"probs{i}", [P, 512]) for i in range(4)]
        probs_t = [sb(f"probs_t{i}", [P, 2, NB, 512]) for i in range(2)]
        context = sb("context", [P, PAIRS, 512])
        row_inv = sb("row_inv", [P, SLOTS])
        vo_tmp = [sb(f"vo_tmp{i}", [P, H0, D]) for i in range(2)]
        h1 = sb("h1", [P, NB, D])
        hid = sb("hid", [P, HB, 512])
        g_max, g_sum, g_inv, g_top = (sb(n, [P, NB]) for n in ("g_max", "g_sum", "g_inv", "g_top"))
        g_off, g_exp, g_key, g_hot, gate = (
            sb(n, [P, NB, E0]) for n in ("g_off", "g_exp", "g_key", "g_hot", "gate"))
        y_tmp = [sb(f"y_tmp{i}", [P, E0, D]) for i in range(2)]
        h2 = sb("h2", [P, NB, D])
        zl_t = sb("zl_t", [P, 2, 512], F16)
        v_l = sb("v_l", [P, NB, D])
        att_t = sb("att_t", [P, NB, 512])
        av_tmp = sb("av_tmp", [P, NB, D])
        h3 = sb("h3", [P, NB, D])
        r_hid = sb("r_hid", [RH, 512])
        r_max, r_sum, r_inv, r_top, r_top2, r_second, r_gap, r_e2, r_den, r_w1, r_w2 = (
            sb(n, [P, NB]) for n in ("r_max", "r_sum", "r_inv", "r_top", "r_top2", "r_second",
                                     "r_gap", "r_e2", "r_den", "r_w1", "r_w2"))
        r_off, r_exp, r_p, r_key, r_hot, r_rest, r_is2, r_key2, r_hot2, r_g1, r_g2, r_gate = (
            sb(n, [P, NB, E1]) for n in ("r_off", "r_exp", "r_p", "r_key", "r_hot", "r_rest", "r_is2",
                                         "r_key2", "r_hot2", "r_g1", "r_g2", "r_gate"))
        e1_t = sb("e1_t", [P, EP, 512])
        e2_t = sb("e2_t", [P, EP, 512])
        o_tmp = [sb(f"o_tmp{i}", [P, E1, D]) for i in range(2)]
        out_sb = sb("out_sb", [P, NB, D])

        s_bank = [ps(f"s_bank{i}") for i in range(3)]
        t_bank = [ps(f"t_bank{i}") for i in range(2)]
        c_bank = ps("c_bank")
        g_bank = [ps(f"g_bank{i}") for i in range(2)]

        zeroed = sem("zeroed")
        weights_in = sem("weights_in")
        consts_made = sem("consts_made")
        pool_setup = sem("pool_setup")
        dve_setup = sem("dve_setup")
        folded = sem("folded")
        wo_ready = sem("wo_ready")
        amax_ready = sem("amax_ready")
        sigma_ready = sem("sigma_ready")
        bn_var = sem("bn_var")
        bn_pow = sem("bn_pow")
        rows_split = sem("rows_split")
        rows_in = sem("rows_in")
        ready = sem("ready")

        x_loaded = signal("x_loaded", 1, 16)
        stored = signal("stored", 2, 16)
        x_turned = signal("x_turned")
        conv_done = signal("conv_done")
        rows1_turned = signal("rows1_turned")
        heads_projected = signal("heads_projected", H0)
        scores_ready = signal("scores_ready", SLOTS)
        probs_turned = signal("probs_turned", SLOTS)
        contexts_ready = signal("contexts_ready", PAIRS)
        attended = signal("attended", NB)
        rows2_turned = signal("rows2_turned")
        hidden_ready = signal("hidden_ready", HB)
        gate_logits = signal("gate_logits")
        experts0_ready = signal("experts0_ready", NB)
        rows3_turned = signal("rows3_turned")
        late_projected = signal("late_projected")
        values_ready = signal("values_ready")
        logits_ready = signal("logits_ready", NB)
        late_contexts = signal("late_contexts")
        rows4_turned = signal("rows4_turned")
        router_hidden = signal("router_hidden")
        router_logits = signal("router_logits")
        layer1_ready = signal("layer1_ready", EP)
        layer2_ready = signal("layer2_ready", EP)
        experts1_ready = signal("experts1_ready", NB)
        x_turned_in = signal("x_turned_in")
        rows1_in = signal("rows1_in")
        heads_hi_in = signal("heads_hi_in", H0)
        probs_ready = signal("probs_ready", SLOTS)
        probs_turned_in = signal("probs_turned_in", SLOTS)
        contexts_in = signal("contexts_in", PAIRS)
        rows2_in = signal("rows2_in")
        hidden_in = signal("hidden_in", HB)
        gate_exp = signal("gate_exp")
        rows3_in = signal("rows3_in")
        late_hi_in = signal("late_hi_in")
        values_in = signal("values_in")
        rows4_in = signal("rows4_in")
        router_hidden_in = signal("router_hidden_in")
        router_exp = signal("router_exp", 2)
        layer2_in = signal("layer2_in", EP)
        signs_ready = signal("signs_ready")
        conv_in = signal("conv_in")
        var1_ready = signal("var1_ready")
        var2_ready = signal("var2_ready")
        var3_ready = signal("var3_ready")
        var4_ready = signal("var4_ready")
        parts1_ready = signal("parts1_ready")
        parts2_ready = signal("parts2_ready")
        parts3_ready = signal("parts3_ready")
        parts4_ready = signal("parts4_ready")
        heads_lo_in = signal("heads_lo_in", H0)
        max_ready = signal("max_ready", SLOTS)
        sums_inverted = signal("sums_inverted")
        attended_in = signal("attended_in", NB)
        gate_offsets = signal("gate_offsets")
        gate_ready = signal("gate_ready")
        experts0_in = signal("experts0_in", NB)
        late_lo_in = signal("late_lo_in")
        logits_in = signal("logits_in", NB)
        late_contexts_in = signal("late_contexts_in")
        h3_ready = signal("h3_ready")
        router_offsets = signal("router_offsets")
        gap_ready = signal("gap_ready")
        route_ready = signal("route_ready")
        layer1_in = signal("layer1_in", EP)
        experts1_in = signal("experts1_in", NB)
        shift_ready = signal("shift_ready", SLOTS)
        factor1_ready = signal("factor1_ready")
        factor2_ready = signal("factor2_ready")
        factor3_ready = signal("factor3_ready")
        factor4_ready = signal("factor4_ready")
        h1_ready = signal("h1_ready", NB)
        h2_ready = signal("h2_ready", NB)
        out_ready = signal("out_ready", NB)
        var_ready = [None, var1_ready, var2_ready, var3_ready, var4_ready]
        parts_ready = [None, parts1_ready, parts2_ready, parts3_ready, parts4_ready]
        factor_ready = [None, factor1_ready, factor2_ready, factor3_ready, factor4_ready]
        rows_turned = [None, rows1_turned, rows2_turned, rows3_turned, rows4_turned]
        ve_front = Chain(sem("ve_front"), 8)
        ve_mid = Chain(sem("ve_mid"), 20)
        ve_late = Chain(sem("ve_late"), 25)
        po_mid = Chain(sem("po_mid"), 3 * NB + 3 * NB)
        po_late = Chain(sem("po_late"), 3 * NB)

        READ_OUT = {
            "xq": x_turned_in, "conv": conv_in, "xt1": rows1_in, "z": heads_lo_in, "vo": attended_in,
            "xt2": rows2_in, "hid": hidden_in, "gate": gate_offsets, "y": experts0_in,
            "xt3": rows3_in, "zl": late_lo_in, "vl": values_in, "lg": logits_in, "av": late_contexts_in,
            "xt4": rows4_in, "rh": router_hidden_in, "rl": router_offsets, "e1": layer1_in, "e2": layer2_in,
            "o": experts1_in}

        def active(i, stage):
            return not isinstance(i, int) or 0 <= i - LAG[stage] < B

        def last_use(i, at):
            j, p = i, at
            while True:
                p -= 2
                if p < 0:
                    j, p = j - 1, p + len(TURNS)
                if isinstance(j, int) and j < 0:
                    return zeroed, 3
                _, stage, what, k = TURNS[p]
                if active(j, stage):
                    read = READ_OUT[what]
                    return read.sem, read.at(j - LAG[stage], k)

        def turns_of(n):
            return [(at, stage, what, k) for at, (slot, stage, what, k) in enumerate(TURNS) if slot == n]

        def each_iteration(eng, body):
            first = max(LAG.values()) + 1
            for i in range(first):
                body(i, i % 2)
            with eng.Fori(first // 2, B // 2) as two:
                body(two * 2, 0)
                body(two * 2 + 1, 1)
            for i in range(B, STEPS):
                body(i, i % 2)

        LOADS = 5 + 12 + 3 + HB + 4 + 2 + 2 * NB + 10
        block = ctx.enter_context(nc.Block())

        @block.sync
        def _(sp):
            n = 0

            def load(dst, src):
                nonlocal n
                sp.dma_start(dst, src).then_inc(weights_in, 16)
                n += 1

            with nc.allow_non_contiguous_dma(reason="weights, once"):
                load(k_raw0[:], kern.rearrange("k c o -> c k o"))
                for i, v in enumerate((bias, mean, var, beta)):
                    load(bn_raw[:, i, :], v.partition_broadcast(P))
                for c in range(2):
                    load(q_dup[:, :, c, :], Q.rearrange("h r d -> r h d"))
                    load(wq_dup[:, c, :], Wq)
                    load(wv_dup[:, c, :], Wv)
                    half = w_raw[D * c:D * c + D, :]
                    load(half[:, W_HID:W_Z], W1)
                    load(half[:, W_R:W_E], rw1)
                    load(half[:, W_E:W_ALL].rearrange("d (e h) -> d e h", e=E1),
                         ew1.rearrange("e d h -> d e h"))
                load(k_raw[:], K.rearrange("h r d -> r h d"))
                load(wk_raw[:], Wk)
                load(wo_raw[:], Wo)
                for m in range(HB):
                    load(wd_w[:, m, :].rearrange("j (e c) -> j e c", e=E0),
                         Wd[:, m * P:(m + 1) * P, :].rearrange("e j c -> j e c"))
                load(wg_w[:], Wg.rearrange("(m j) e -> j m e", m=HB))
                load(b1_c[:], b1.rearrange("(m j) -> j m", m=HB))
                load(rw2_w[:], rw2)
                load(rb1_c[:], rb1.rearrange("(r o) -> r o", o=1))
                load(row[:, R_D:R_3], bd.rearrange("(o e) c -> o (e c)", o=1))
                load(row[:, R_3:R_G], eb3.rearrange("(o e) c -> o (e c)", o=1))
                for t in range(NB):
                    load(row[:, R_G + t * E0:R_G + (t + 1) * E0], bg.rearrange("(o e) -> o e", o=1))
                    load(row[:, R_L + t * E1:R_L + (t + 1) * E1], rb2.rearrange("(o e) -> o e", o=1))
                sp.wait_ge(zeroed, 3)
                for c in range(2):
                    half = slice(D * c, D * c + D)
                    load(vo_w[half, :, half], VO.rearrange("(p s) d e -> s d p e", s=2)[c])
                    load(e2_w[half, :, half], ew2.rearrange("(p s) d e -> s d p e", s=2)[c])
                    load(e3_w[half, :, half], ew3.rearrange("(p s) d e -> s d p e", s=2)[c])
                    load(eb1_c[half, :], eb1.rearrange("(p s) h -> s h p", s=2)[c])
                    load(eb2_c[half, :], eb2.rearrange("(p s) h -> s h p", s=2)[c])
            assert n == LOADS, n
            sp.wait_ge(rows_split, 1)
            for r in range(3):
                sp.dma_start(bias_rows[r:r + 1, :], row_part[:, r, :]).then_inc(rows_in, 16)

            def body(i, parity):
                if active(i, "front"):
                    b = i
                    if begun(b - 1):
                        sp.wait_ge(signs_ready.sem, signs_ready.at(b - 1))
                    sp.dma_start(x_in[:], x[b].rearrange("(n p) c -> p n c", p=P)).then_inc(x_loaded.sem, 16)
                if active(i, "late"):
                    b = i - LAG["late"]
                    sp.wait_ge(out_ready.sem, out_ready.at(b, NB - 1))
                    sp.dma_start(out[b, 0:T - TAIL, :].rearrange("(n p) c -> p n c", p=P),
                                 out_sb[:, 0:NB - 1, :]).then_inc(stored.sem, 16)
                    sp.dma_start(out[b, T - TAIL:T, :], out_sb[0:TAIL, NB - 1, :]).then_inc(stored.sem, 16)

            each_iteration(sp, body)
            sp.wait_ge(stored.sem, stored.at(B - 1, 1))

        @block.gpsimd
        def _(pool):
            g = nc.gpsimd
            for t in (vo_w, e2_w, e3_w):
                g.memset(t[:], 0.0).then_inc(zeroed, 1)
            n = 0

            def link(ins):
                nonlocal n
                ins.then_inc(pool_setup, 1)
                n += 1
                pool.wait_ge(pool_setup, n)

            for t in (id32, id16, idb):
                link(g.memset(t[:], 0.0))
                link(g.affine_select(out=t[:], in_=t[:], compare_op=ALU.not_equal, fill=1.0, base=0,
                                     pattern=[[-1, P]], channel_multiplier=1))
            link(g.memset(causal[:], 1.0))
            link(g.affine_select(out=causal[:], in_=causal[:], compare_op=ALU.is_ge, fill=0.0, base=0,
                                 pattern=[[1, 512]], channel_multiplier=-1))
            link(g.iota(row_no[:], pattern=[[P, NB]], base=0, channel_multiplier=1))
            link(g.iota(rank_i[:], pattern=[[-1, E0]], base=E0, channel_multiplier=0))
            link(g.memset(minus_half[:], -0.5))
            link(g.memset(bn_exp[:], -0.5))
            link(g.memset(ones_rows[:], 1.0))
            link(g.memset(xq_t[:, T_IN:], 0.0))
            for t in probs:
                link(g.memset(t[:, T:], 0.0))
            g.memset(xq_t[:, 0:T_IN], 0.0).then_inc(consts_made, 1)
            pool.wait_ge(bn_var, 1)
            g.tensor_tensor(bn_inv[:], bn_raw[:, 2, :], bn_exp[:], ALU.pow).then_inc(bn_pow, 1)
            pool.wait_ge(amax_ready, 1)
            g.partition_all_reduce(sigma[:], amax[:], P, bass.bass_isa.ReduceOp.max).then_inc(sigma_ready, 1)
            pool.wait_ge(ready, 1)

            def inverse_root(stage, i, b):
                pool.wait_ge(var_ready[stage].sem, var_ready[stage].at(b))
                g.tensor_tensor(ln[stage - 1]["r"][:], ln[stage - 1]["var"][:], minus_half[:],
                                ALU.pow).then_inc(factor_ready[stage].sem, 1)

            def tree(chain, b, t, n_parts, last_in, last_out, last_sem):
                if n_parts == 8:
                    chain.link(pool, b, g.tensor_tensor(t[:, 0:4], t[:, 0:4], t[:, 4:8], ALU.add))
                    chain.link(pool, b, g.tensor_tensor(t[:, 0:2], t[:, 0:2], t[:, 2:4], ALU.add))
                else:
                    chain.link(pool, b, g.tensor_tensor(t[:, 0:3], t[:, 0:3], t[:, 3:6], ALU.add))
                    chain.link(pool, b, g.tensor_tensor(t[:, 1], t[:, 1], t[:, 2], ALU.add))
                chain.link(pool, b, g.tensor_tensor(t[:, 0], t[:, 0], t[:, 1], ALU.add))
                g.tensor_tensor(last_out, t[:, 0], last_in, ALU.add).then_inc(last_sem, 1)

            def body(i, parity):
                for n in range(SLOTS):
                    if active(i, "attn"):
                        b = i - LAG["attn"]
                        pool.wait_ge(max_ready.sem, max_ready.at(b, n))
                        g.tensor_tensor(exp_bias[:, n:n + 1], neg_max[:, n:n + 1],
                                        exp_scale[:, n // NB:n // NB + 1], ALU.mult).then_inc(shift_ready.sem, 1)
                    if active(i, "mid"):
                        b = i - LAG["mid"]
                        if 8 <= n < 8 + NB:
                            t = n - 8
                            pool.wait_ge(attended_in.sem, attended_in.at(b, t))
                            tree(po_mid, b, vo_tmp[t % 2], 8, h0[parity][:, t], h1[:, t], h1_ready.sem)
                        if 24 <= n < 24 + NB:
                            t = n - 24
                            pool.wait_ge(experts0_in.sem, experts0_in.at(b, t))
                            if t == 0:
                                if begun(b - 1):
                                    pool.wait_ge(h3_ready.sem, h3_ready.at(b - 1))
                            tree(po_mid, b, y_tmp[t % 2], 8, h1[:, t], h2[:, t], h2_ready.sem)
                        if n == 13:
                            inverse_root(2, i, b)
                        if n == 29:
                            inverse_root(3, i, b)
                    if active(i, "late"):
                        b = i - LAG["late"]
                        if n == 15:
                            inverse_root(4, i, b)
                        if 28 <= n < 28 + NB:
                            t = n - 28
                            pool.wait_ge(experts1_in.sem, experts1_in.at(b, t))
                            if t == 0:
                                if begun(b - 1):
                                    pool.wait_ge(stored.sem, stored.at(b - 1, 1))
                            tree(po_late, b, o_tmp[t % 2], 6, h3[:, t], out_sb[:, t], out_ready.sem)
                    if active(i, "front") and n == 17:
                        inverse_root(1, i, i)
                if active(i, "mid"):
                    po_mid.end()
                if active(i, "late"):
                    po_late.end()

            each_iteration(pool, body)

        @block.scalar
        def _(act):
            a = nc.scalar
            act.wait_ge(ready, 1)

            def store_turn(i, parity, at, stage, what, k):
                b = i - LAG[stage]
                G = g_bank[at % 2]
                if what == "xq":
                    act.wait_ge(x_turned.sem, x_turned.at(b))
                    if begun(b - 1):
                        act.wait_ge(conv_done.sem, conv_done.at(b - 1))
                    a.activation(xq_t[:, 0:T_IN], G[:].bitcast(BF16)[:, 0:T_IN], ACT.Copy).then_inc(x_turned_in.sem, 1)
                elif what == "xt1":
                    act.wait_ge(rows1_turned.sem, rows1_turned.at(b))
                    if begun(b - 2):
                        act.wait_ge(scores_ready.sem, scores_ready.at(b - 2, SLOTS - 1))
                    a.activation(xt1[parity][:], G[:].bitcast(F16)[:, 0:512], ACT.Copy).then_inc(rows1_in.sem, 1)
                elif what == "xt2":
                    act.wait_ge(rows2_turned.sem, rows2_turned.at(b))
                    if begun(b - 1):
                        act.wait_ge(hidden_ready.sem, hidden_ready.at(b - 1, HB - 1))
                    a.activation(xt2[:], G[:].bitcast(F16)[:, 0:512], ACT.Copy).then_inc(rows2_in.sem, 1)
                elif what == "xt3":
                    act.wait_ge(rows3_turned.sem, rows3_turned.at(b))
                    if begun(b - 1):
                        act.wait_ge(logits_ready.sem, logits_ready.at(b - 1, NB - 1))
                    a.activation(xt3[:], G[:].bitcast(F16)[:, 0:512], ACT.Copy).then_inc(rows3_in.sem, 1)
                elif what == "xt4":
                    act.wait_ge(rows4_turned.sem, rows4_turned.at(b))
                    if begun(b - 1):
                        act.wait_ge(layer1_ready.sem, layer1_ready.at(b - 1, EP - 1))
                    a.activation(xt4[:], G[:].bitcast(F16)[:, 0:512], ACT.Copy).then_inc(rows4_in.sem, 1)
                elif what == "z":
                    act.wait_ge(heads_projected.sem, heads_projected.at(b, k))
                    past, which_k = scores_ready.before(b, NB * k + NB - 1, 2 * NB)
                    if begun(past):
                        act.wait_ge(scores_ready.sem, scores_ready.at(past, which_k))
                    a.activation(z_t[k % 2][:, 0, :], G[:], ACT.Copy, scale=ZS).then_inc(heads_hi_in.sem, 1)
                elif what == "zl":
                    act.wait_ge(late_projected.sem, late_projected.at(b))
                    if begun(b - 1):
                        act.wait_ge(logits_ready.sem, logits_ready.at(b - 1, NB - 1))
                    a.activation(zl_t[:, 0, :], G[:], ACT.Copy, scale=ZS).then_inc(late_hi_in.sem, 1)
                elif what == "vl":
                    act.wait_ge(values_ready.sem, values_ready.at(b))
                    if begun(b - 1):
                        act.wait_ge(late_contexts.sem, late_contexts.at(b - 1))
                    a.activation(v_l[:].rearrange("p n d -> p (n d)"), G[:, 0:NB * D], ACT.Copy).then_inc(values_in.sem, 1)
                elif what == "hid" and k == HB - 1:
                    if begun(b - 1):
                        act.wait_ge(experts0_ready.sem, experts0_ready.at(b - 1, NB - 1))
                    for m in range(HB):
                        act.wait_ge(hidden_ready.sem, hidden_ready.at(b, m))
                        a.activation(hid[:, m, :], g_bank[(at - (HB - 1 - m)) % 2][:], ACT.Gelu,
                                     bias=b1_c[:, m:m + 1], scale=hid_scale[:, 0:1]).then_inc(hidden_in.sem, 1)
                elif what == "rh":
                    act.wait_ge(router_hidden.sem, router_hidden.at(b))
                    if begun(b - 1):
                        act.wait_ge(router_logits.sem, router_logits.at(b - 1))
                    a.activation(r_hid[:], G[0:RH, :], ACT.Relu, bias=rb1_c[:, 0:1]).then_inc(router_hidden_in.sem, 1)
                elif what == "e2":
                    act.wait_ge(layer2_ready.sem, layer2_ready.at(b, k))
                    if begun(b - 1):
                        act.wait_ge(experts1_ready.sem, experts1_ready.at(b - 1, NB - 1))
                    a.activation(e2_t[:, k, :], G[:], ACT.Relu, bias=eb2_c[:, k:k + 1]).then_inc(layer2_in.sem, 1)

            def exp(b, par, m):
                act.wait_ge(shift_ready.sem, shift_ready.at(b, m))
                past, which_k = probs_turned.before(b, m, 4)
                if begun(past):
                    act.wait_ge(probs_turned.sem, probs_turned.at(past, which_k))
                if m == 0:
                    if begun(b - 2):
                        act.wait_ge(sums_inverted.sem, sums_inverted.at(b - 2))
                a.activation(probs[m % 4][:, 0:T], s_bank[m % 3][:, 0:T], ACT.Exp,
                             bias=exp_bias[:, m:m + 1], scale=exp_scale[:, m // NB:m // NB + 1],
                             accum_out=row_sum[par][:, m:m + 1]).then_inc(probs_ready.sem, 1)

            def store_probs_t(b, m):
                h, t, p = m // NB, m % NB, m // (2 * NB)
                act.wait_ge(probs_turned.sem, probs_turned.at(b, m))
                if m % (2 * NB) == 0:
                    past, which_k = contexts_ready.before(b, p, 2)
                    if begun(past):
                        act.wait_ge(contexts_ready.sem, contexts_ready.at(past, which_k))
                a.activation(probs_t[p % 2][:, h % 2, :, t * P:(t + 1) * P],
                             t_bank[m % 2][:].rearrange("p (j t) -> p j t", j=NB), ACT.Copy).then_inc(probs_turned_in.sem, 1)

            def store_context(b, p):
                act.wait_ge(contexts_ready.sem, contexts_ready.at(b, p))
                if begun(b - 1):
                    act.wait_ge(attended.sem, attended.at(b - 1, NB - 1))
                a.activation(context[:, p, :], c_bank[:], ACT.Copy).then_inc(contexts_in.sem, 1)

            def body(i, parity):
                for n in range(SLOTS):
                    mine = turns_of(n)
                    before, after = mine[:1], mine[1:]
                    for turn in before:
                        if active(i, turn[1]):
                            store_turn(i, parity, *turn)
                    if n >= 1 and active(i, "attn"):
                        exp(i - 1, 1 - parity, n - 1)
                    if n == 0 and active(i, "mid"):
                        exp(i - 2, parity, SLOTS - 1)
                    for turn in after:
                        if active(i, turn[1]):
                            store_turn(i, parity, *turn)
                    if n >= 3 and active(i, "attn"):
                        store_probs_t(i - 1, n - 3)
                    if n < 3 and active(i, "mid"):
                        store_probs_t(i - 2, SLOTS + n - 3)
                    if n in (15, 23, 31) and active(i, "attn"):
                        store_context(i - 1, n // 8 - 1)
                    if n == 7 and active(i, "mid"):
                        store_context(i - 2, PAIRS - 1)
                    if n == 23 and active(i, "mid"):
                        act.wait_ge(gate_offsets.sem, gate_offsets.at(i - 2))
                        a.activation(g_exp[:], g_off[:], ACT.Exp).then_inc(gate_exp.sem, 1)
                    if n == 24 and active(i, "late"):
                        act.wait_ge(router_offsets.sem, router_offsets.at(i - 3))
                        a.activation(r_exp[:], r_off[:], ACT.Exp).then_inc(router_exp.sem, 1)
                    if n == 25 and active(i, "late"):
                        act.wait_ge(gap_ready.sem, gap_ready.at(i - 3))
                        a.activation(r_e2[:], r_gap[:], ACT.Exp).then_inc(router_exp.sem, 1)

            each_iteration(act, body)

        @block.vector
        def _(dve):
            v = nc.vector
            n_setup = 0

            def setup(ins):
                nonlocal n_setup
                ins.then_inc(dve_setup, 1)
                n_setup += 1
                dve.wait_ge(dve_setup, n_setup)

            def over(ap, shape):
                return ap.broadcast_to(shape)

            dve.wait_ge(weights_in, 16 * LOADS)
            dve.wait_ge(consts_made, 1)
            v.tensor_scalar(bn_raw[:, 2, :], bn_raw[:, 2, :], BN_EPS, None, ALU.add).then_inc(bn_var, 1)
            setup(v.tensor_tensor(bn_raw[:, 0, :], bn_raw[:, 0, :], bn_raw[:, 1, :], ALU.subtract))
            setup(v.tensor_scalar(k_sign[:], k_raw0[:], 0.0, 0.5, ALU.is_ge, ALU.subtract))
            dve.wait_ge(bn_pow, 1)
            setup(v.tensor_scalar(bn_scale[:], bn_inv[:], 4.0, None, ALU.mult))
            setup(v.tensor_tensor(bn_shift[:], bn_raw[:, 0, :], bn_inv[:], ALU.mult))
            setup(v.tensor_tensor(bn_shift[:], bn_shift[:], bn_raw[:, 3, :], ALU.add))
            setup(v.tensor_copy(row_part[:, 0, :], row[:]))
            setup(v.tensor_tensor(row_rest[:, 0, :], row[:], row_part[:, 0, :], ALU.subtract))
            setup(v.tensor_copy(row_part[:, 1, :], row_rest[:, 0, :]))
            setup(v.tensor_tensor(row_rest[:, 1, :], row_rest[:, 0, :], row_part[:, 1, :], ALU.subtract))
            v.tensor_copy(row_part[:, 2, :], row_rest[:, 1, :]).then_inc(rows_split, 1)
            dve.wait_ge(folded, 1)
            v.tensor_copy(wo_t[:], s_bank[2][0:D, 0:D]).then_inc(wo_ready, 1)
            dve.wait_ge(folded, 2)
            setup(v.tensor_copy(w_raw[:, W_Z:W_R], s_bank[1][:, 0:2 * D]))
            for s, (lo, hi) in enumerate(SEGMENTS):
                setup(v.tensor_reduce(amax[:, H0 + s:H0 + s + 1], w_raw[:, lo:hi], axis=AX, op=ALU.max,
                                      apply_absolute_value=True))
            heads = s_bank[0][:].rearrange("p (h d) -> p h d", h=H0)
            v.tensor_reduce(amax[:, 0:H0], heads, axis=AX, op=ALU.max,
                            apply_absolute_value=True).then_inc(amax_ready, 1)
            dve.wait_ge(sigma_ready, 1)
            setup(v.tensor_scalar(sigma[:], sigma[:], TINY, None, ALU.max))
            setup(v.reciprocal(rsigma[:], sigma[:]))
            setup(v.tensor_scalar(unscale[:], sigma[:], 1.0 / LIN, None, ALU.mult))
            setup(v.tensor_scalar(rescale[:], rsigma[:], LIN, None, ALU.mult))
            setup(v.tensor_scalar(exp_scale[:], sigma[:, 0:H0], 1.0 / (LOGIT * D ** 0.5), None, ALU.mult))
            setup(v.tensor_copy(hid_scale[:], unscale[:, SG_HID:SG_HID + 1]))
            setup(v.tensor_scalar(rsigma[:], rsigma[:], WS, None, ALU.mult))
            setup(v.tensor_tensor(a_nrm[:], heads, over(rsigma[:, 0:H0, None], [P, H0, D]), ALU.mult))
            for s, (lo, hi) in enumerate(SEGMENTS):
                setup(v.tensor_scalar(w_nrm[:, lo:hi], w_raw[:, lo:hi], rsigma[:, H0 + s:H0 + s + 1], None, ALU.mult))
            setup(v.tensor_copy(w_hi[:], w_nrm[:]))
            setup(v.tensor_tensor(w_lo[:], w_nrm[:], w_hi[:], ALU.subtract))
            for c in range(2):
                setup(v.tensor_copy(a_w[:, :, 0, c, :], a_nrm[:]))
                setup(v.tensor_tensor(a_w[:, :, 1, c, :], a_nrm[:], a_w[:, :, 0, c, :], ALU.subtract))
                setup(v.tensor_copy(z_w[:, 0, c, :], w_hi[:, W_Z:W_V]))
                setup(v.tensor_copy(z_w[:, 1, c, :], w_lo[:, W_Z:W_V]))
            setup(v.tensor_scalar(vo_w[:], vo_w[:], 1.0 / XS, None, ALU.mult))
            setup(v.tensor_scalar(rb1_c[:], rb1_c[:], rescale[0:RH, SG_R:SG_R + 1], None, ALU.mult))
            setup(v.tensor_scalar(rw2_w[:], rw2_w[:], unscale[0:RH, SG_R:SG_R + 1], None, ALU.mult))
            setup(v.tensor_scalar(eb1_c[:], eb1_c[:], rescale[:, SG_E:SG_E + 1], None, ALU.mult))
            setup(v.tensor_scalar(e2_w[:], e2_w[:], unscale[:, SG_E:SG_E + 1], None, ALU.mult))
            setup(v.tensor_copy(row_scale[:], row_no[:]))
            setup(v.tensor_scalar(row_scale[:], row_scale[:], 1.0, None, ALU.max))
            setup(v.reciprocal(row_scale[:], row_scale[:]))
            setup(v.tensor_scalar(row_scale[:], row_scale[:], sigma[:, SG_Z:SG_Z + 1], 1.0 / LOGIT, ALU.mult, ALU.mult))
            setup(v.tensor_scalar(row_scale[:], row_scale[:], unscale[:, SG_V:SG_V + 1], None, ALU.mult))
            setup(v.tensor_copy(rank[:], rank_i[:]))
            dve.wait_ge(rows_in, 48)
            v.tensor_copy(g_max[:], row_scale[:]).then_inc(ready, 1)

            def ln_stats(chain, b, which, src):
                w = ln[which - 1]
                chain.link(dve, b, v.reduce_sum(w["sum"][:], src[:], axis=AX))
                chain.link(dve, b, v.tensor_scalar(w["mu"][:], w["sum"][:], -1.0 / D, None, ALU.mult))
                chain.link(dve, b, v.tensor_tensor(w["d"][:], src[:], over(w["mu"][:, :, None], [P, NB, D]), ALU.add))
                chain.link(dve, b, v.tensor_tensor(w["sq"][:], w["d"][:], w["d"][:], ALU.mult))
                chain.link(dve, b, v.reduce_sum(w["sum2"][:], w["sq"][:], axis=AX))
                v.tensor_scalar(w["var"][:], w["sum2"][:], 1.0 / (D * XS * XS), LN_EPS / (XS * XS),
                                ALU.mult, ALU.add).then_inc(var_ready[which].sem, 1)

            def ln_parts(chain, b, which, dst):
                w = ln[which - 1]
                dve.wait_ge(factor_ready[which].sem, factor_ready[which].at(b))
                if begun(b - 1):
                    dve.wait_ge(rows_turned[which].sem, rows_turned[which].at(b - 1))
                chain.link(dve, b, v.tensor_tensor(dst[:], w["d"][:], over(w["r"][:, :, None], [P, NB, D]), ALU.mult))
                chain.link(dve, b, v.tensor_copy(w["parts"][:, :, 0:D], dst[:]))
                v.tensor_tensor(w["parts"][:, :, D:2 * D], dst[:], w["parts"][:, :, 0:D],
                                ALU.subtract).then_inc(parts_ready[which].sem, 1)

            def ranked(n):
                return over(rank[:, None, 0:n], [P, NB, n])

            def store_turn(i, parity, at, stage, what, k):
                b = i - LAG[stage]
                G = g_bank[at % 2]
                if what == "z":
                    dve.wait_ge(heads_hi_in.sem, heads_hi_in.at(b, k))
                    v.scalar_tensor_tensor(out=z_t[k % 2][:, 1, :], in0=G[:], scalar=ZS, in1=z_t[k % 2][:, 0, :],
                                           op0=ALU.mult, op1=ALU.subtract).then_inc(heads_lo_in.sem, 1)
                elif what == "zl":
                    dve.wait_ge(late_hi_in.sem, late_hi_in.at(b))
                    v.scalar_tensor_tensor(out=zl_t[:, 1, :], in0=G[:], scalar=ZS, in1=zl_t[:, 0, :],
                                           op0=ALU.mult, op1=ALU.subtract).then_inc(late_lo_in.sem, 1)
                elif what == "conv":
                    dve.wait_ge(conv_done.sem, conv_done.at(b))
                    if begun(b - 2):
                        dve.wait_ge(h1_ready.sem, h1_ready.at(b - 2, NB - 1))
                    h = h0[parity]
                    v.tensor_tensor(h[:], G[:, 0:NB * D].rearrange("p (n d) -> p n d", n=NB),
                                    over(bn_scale[:, None, :], [P, NB, D]), ALU.mult).then_inc(conv_in.sem, 1)
                    dve.wait_ge(conv_in.sem, conv_in.at(b))
                    ve_front.link(dve, b, v.tensor_tensor(h[:], h[:], over(bn_shift[:, None, :], [P, NB, D]), ALU.add))
                elif what == "vo":
                    dve.wait_ge(attended.sem, attended.at(b, k))
                    past, which_k = h1_ready.before(b, k, 2)
                    if begun(past):
                        dve.wait_ge(h1_ready.sem, h1_ready.at(past, which_k))
                    inv = row_inv[:].rearrange("p (h t) -> p h t", h=H0)[:, :, k:k + 1]
                    v.tensor_tensor(vo_tmp[k % 2][:], G[:].rearrange("p (h d) -> p h d", h=H0),
                                    over(inv, [P, H0, D]), ALU.mult).then_inc(attended_in.sem, 1)
                elif what == "gate":
                    dve.wait_ge(gate_logits.sem, gate_logits.at(b))
                    logits = G[:, 0:NB * E0].rearrange("p (n e) -> p n e", n=NB)
                    ve_mid.link(dve, b, v.reduce_max(g_max[:], logits, axis=AX))
                    v.tensor_tensor(g_off[:], logits, over(g_max[:, :, None], [P, NB, E0]),
                                    ALU.subtract).then_inc(gate_offsets.sem, 1)
                elif what == "y":
                    dve.wait_ge(experts0_ready.sem, experts0_ready.at(b, k))
                    past, which_k = h2_ready.before(b, k, 2)
                    if begun(past):
                        dve.wait_ge(h2_ready.sem, h2_ready.at(past, which_k))
                    if k == 0:
                        dve.wait_ge(gate_ready.sem, gate_ready.at(b))
                    v.tensor_tensor(y_tmp[k % 2][:], G[:].rearrange("p (e d) -> p e d", e=E0),
                                    over(gate[:, k, :, None], [P, E0, D]), ALU.mult).then_inc(experts0_in.sem, 1)
                elif what == "lg":
                    dve.wait_ge(logits_ready.sem, logits_ready.at(b, k))
                    if k == 0:
                        if begun(b - 1):
                            dve.wait_ge(late_contexts.sem, late_contexts.at(b - 1))
                    wide = 512 - k * P
                    v.scalar_tensor_tensor(out=att_t[:, k, k * P:512], in0=G[:, 0:wide], scalar=0.0,
                                           in1=causal[:, 0:wide], op0=ALU.max, op1=ALU.mult).then_inc(logits_in.sem, 1)
                elif what == "av":
                    dve.wait_ge(late_contexts.sem, late_contexts.at(b))
                    v.tensor_tensor(av_tmp[:], G[:, 0:NB * D].rearrange("p (n d) -> p n d", n=NB),
                                    over(row_scale[:, :, None], [P, NB, D]), ALU.mult).then_inc(late_contexts_in.sem, 1)
                    dve.wait_ge(late_contexts_in.sem, late_contexts_in.at(b))
                    if begun(b - 1):
                        dve.wait_ge(out_ready.sem, out_ready.at(b - 1, NB - 1))
                    dve.wait_ge(h2_ready.sem, h2_ready.at(b, NB - 1))
                    v.tensor_tensor(h3[:], av_tmp[:], h2[:], ALU.add).then_inc(h3_ready.sem, 1)
                    dve.wait_ge(h3_ready.sem, h3_ready.at(b))
                elif what == "rl":
                    dve.wait_ge(router_logits.sem, router_logits.at(b))
                    logits = G[:, 0:NB * E1].rearrange("p (n e) -> p n e", n=NB)
                    ve_late.link(dve, b, v.reduce_max(r_max[:], logits, axis=AX))
                    v.tensor_tensor(r_off[:], logits, over(r_max[:, :, None], [P, NB, E1]),
                                    ALU.subtract).then_inc(router_offsets.sem, 1)
                elif what == "e1":
                    dve.wait_ge(layer1_ready.sem, layer1_ready.at(b, k))
                    if begun(b - 1):
                        dve.wait_ge(layer2_ready.sem, layer2_ready.at(b - 1, k))
                    v.tensor_scalar(e1_t[:, k, :], G[:], eb1_c[:, k:k + 1], 0.0, ALU.add, ALU.max).then_inc(layer1_in.sem, 1)
                elif what == "o":
                    dve.wait_ge(experts1_ready.sem, experts1_ready.at(b, k))
                    past, which_k = out_ready.before(b, k, 2)
                    if begun(past):
                        dve.wait_ge(out_ready.sem, out_ready.at(past, which_k))
                    if k == 0:
                        dve.wait_ge(route_ready.sem, route_ready.at(b))
                    v.tensor_tensor(o_tmp[k % 2][:], G[:, 0:E1 * D].rearrange("p (e d) -> p e d", e=E1),
                                    over(r_gate[:, k, :, None], [P, E1, D]), ALU.mult).then_inc(experts1_in.sem, 1)

            def finish_gate(b):
                def link(ins):
                    ve_mid.link(dve, b, ins)
                dve.wait_ge(gate_exp.sem, gate_exp.at(b))
                link(v.reduce_sum(g_sum[:], g_exp[:], axis=AX))
                link(v.reciprocal(g_inv[:], g_sum[:]))
                link(v.scalar_tensor_tensor(out=g_key[:], in0=g_off[:], scalar=0.0, in1=ranked(E0), op0=ALU.is_ge, op1=ALU.mult))
                link(v.reduce_max(g_top[:], g_key[:], axis=AX))
                link(v.tensor_tensor(g_hot[:], g_key[:], over(g_top[:, :, None], [P, NB, E0]), ALU.is_equal))
                v.tensor_tensor(gate[:], g_hot[:], over(g_inv[:, :, None], [P, NB, E0]), ALU.mult).then_inc(gate_ready.sem, 1)

            def route(b):
                def link(ins):
                    ve_late.link(dve, b, ins)
                dve.wait_ge(router_exp.sem, router_exp.at(b, 0))
                link(v.reduce_sum(r_sum[:], r_exp[:], axis=AX))
                link(v.reciprocal(r_inv[:], r_sum[:]))
                link(v.tensor_tensor(r_p[:], r_exp[:], over(r_inv[:, :, None], [P, NB, E1]), ALU.mult))
                link(v.scalar_tensor_tensor(out=r_key[:], in0=r_off[:], scalar=0.0, in1=ranked(E1), op0=ALU.is_ge, op1=ALU.mult))
                link(v.reduce_max(r_top[:], r_key[:], axis=AX))
                link(v.tensor_tensor(r_hot[:], r_key[:], over(r_top[:, :, None], [P, NB, E1]), ALU.is_equal))
                link(v.scalar_tensor_tensor(out=r_rest[:], in0=r_hot[:], scalar=-2.0, in1=r_p[:], op0=ALU.mult, op1=ALU.add))
                link(v.reduce_max(r_second[:], r_rest[:], axis=AX))
                link(v.tensor_tensor(r_is2[:], r_rest[:], over(r_second[:, :, None], [P, NB, E1]), ALU.is_equal))
                link(v.tensor_tensor(r_key2[:], r_is2[:], ranked(E1), ALU.mult))
                link(v.reduce_max(r_top2[:], r_key2[:], axis=AX))
                link(v.tensor_tensor(r_hot2[:], r_key2[:], over(r_top2[:, :, None], [P, NB, E1]), ALU.is_equal))
                v.tensor_tensor(r_gap[:], r_second[:], r_inv[:], ALU.subtract).then_inc(gap_ready.sem, 1)

            def finish_route(b):
                def link(ins):
                    ve_late.link(dve, b, ins)
                dve.wait_ge(router_exp.sem, router_exp.at(b, 1))
                link(v.tensor_scalar(r_den[:], r_e2[:], 1.0, None, ALU.add))
                link(v.reciprocal(r_w1[:], r_den[:]))
                link(v.tensor_tensor(r_w2[:], r_w1[:], r_e2[:], ALU.mult))
                link(v.tensor_tensor(r_g1[:], r_hot[:], over(r_w1[:, :, None], [P, NB, E1]), ALU.mult))
                link(v.tensor_tensor(r_g2[:], r_hot2[:], over(r_w2[:, :, None], [P, NB, E1]), ALU.mult))
                v.tensor_tensor(r_gate[:], r_g1[:], r_g2[:], ALU.add).then_inc(route_ready.sem, 1)

            def body(i, parity):
                for n in range(SLOTS):
                    mine = turns_of(n)
                    before, after = mine[:1], mine[1:]
                    for turn in before:
                        if active(i, turn[1]):
                            store_turn(i, parity, *turn)
                    if active(i, "attn"):
                        b = i - LAG["attn"]
                        dve.wait_ge(scores_ready.sem, scores_ready.at(b, n))
                        v.tensor_reduce(neg_max[:, n:n + 1], s_bank[n % 3][:, 0:T], axis=AX, op=ALU.max,
                                        negate=True).then_inc(max_ready.sem, 1)
                    for turn in after:
                        if active(i, turn[1]):
                            store_turn(i, parity, *turn)
                    if active(i, "front"):
                        if n == 9:
                            dve.wait_ge(x_loaded.sem, x_loaded.at(i))
                            if begun(i - 1):
                                dve.wait_ge(x_turned.sem, x_turned.at(i - 1))
                            v.tensor_scalar(x_sign[:], x_in[:], 0.0, 0.5, ALU.is_ge, ALU.subtract).then_inc(signs_ready.sem, 1)
                        if n == 17:
                            ln_stats(ve_front, i, 1, h0[parity])
                        if n == 18:
                            if begun(i - 2):
                                dve.wait_ge(contexts_ready.sem, contexts_ready.at(i - 2, PAIRS - 1))
                            ln_parts(ve_front, i, 1, xn1[parity])
                    if active(i, "mid"):
                        b = i - LAG["mid"]
                        if n == 2:
                            dve.wait_ge(probs_ready.sem, probs_ready.at(b, SLOTS - 1))
                            v.reciprocal(row_inv[:], row_sum[parity][:]).then_inc(sums_inverted.sem, 1)
                            dve.wait_ge(sums_inverted.sem, sums_inverted.at(b))
                        if n == 13:
                            dve.wait_ge(h1_ready.sem, h1_ready.at(b, NB - 1))
                            ln_stats(ve_mid, b, 2, h1)
                        if n == 14:
                            ln_parts(ve_mid, b, 2, xn_other[0])
                        if n == 23:
                            finish_gate(b)
                        if n == 29:
                            dve.wait_ge(h2_ready.sem, h2_ready.at(b, NB - 1))
                            ln_stats(ve_mid, b, 3, h2)
                        if n == 30:
                            ln_parts(ve_mid, b, 3, xn_other[1])
                    if active(i, "late"):
                        b = i - LAG["late"]
                        if n == 15:
                            ln_stats(ve_late, b, 4, h3)
                        if n == 16:
                            ln_parts(ve_late, b, 4, xn_other[2])
                        if n == 24:
                            route(b)
                        if n == 25:
                            finish_route(b)
                if active(i, "front"):
                    ve_front.end()
                if active(i, "mid"):
                    ve_mid.end()
                if active(i, "late"):
                    ve_late.end()

            each_iteration(dve, body)

        @block.tensor
        def _(pe):
            t_ = nc.tensor

            def product(dst, pairs, start=True):
                for n, (lhs, rhs) in enumerate(pairs):
                    last = t_.matmul(dst, lhs, rhs, start=start and n == 0, stop=n == len(pairs) - 1,
                                     skip_group_check=True)
                return last

            pe.wait_ge(weights_in, 16 * LOADS)
            pe.wait_ge(consts_made, 1)
            t_.transpose(s_bank[2][0:D, 0:D], wo_raw[:], id32[0:D, 0:D]).then_inc(folded, 1)
            for h in range(H0):
                product(s_bank[0][:, h * D:(h + 1) * D], [(q_dup[:, h, :, :].rearrange("r c d -> r (c d)"), k_raw[:, h, :])])
            product(s_bank[1][:, 0:D], [(wq_dup[:].rearrange("c s d -> c (s d)"), wk_raw[:])])
            pe.wait_ge(wo_ready, 1)
            product(s_bank[1][:, D:2 * D], [(wv_dup[:].rearrange("c s d -> c (s d)"), wo_t[:])]).then_inc(folded, 1)
            pe.wait_ge(ready, 1)

            def stacked(lo, hi, xt, lhs=True):
                return [(w[:, lo:hi], xt) if lhs else (xt, w[:, lo:hi]) for w in (w_hi, w_lo)]

            def turn(i, parity, at, stage, what, k):
                b = i - LAG[stage]
                G, read_out = g_bank[at % 2], last_use(i, at)
                blk = slice(k * P, (k + 1) * P)
                if what == "xq":
                    pe.wait_ge(signs_ready.sem, signs_ready.at(b))
                    pe.wait_ge(*read_out)
                    for n in range(NB):
                        last = t_.transpose(G[:].bitcast(BF16)[:, n * P:(n + 1) * P], x_sign[:, n, :], idb[:])
                    last.then_inc(x_turned.sem, 1)
                elif what == "conv":
                    pe.wait_ge(x_turned_in.sem, x_turned_in.at(b))
                    pe.wait_ge(*read_out)
                    for n in range(NB):
                        last = product(G[:, n * D:(n + 1) * D],
                                       [(xq_t[:, n * P + s:n * P + s + P], k_sign[:, s, :]) for s in range(TAPS)])
                    last.then_inc(conv_done.sem, 1)
                elif what in ("xt1", "xt2", "xt3", "xt4"):
                    which = int(what[2])
                    w = ln[which - 1]["parts"]
                    pe.wait_ge(parts_ready[which].sem, parts_ready[which].at(b))
                    pe.wait_ge(*read_out)
                    for n in range(NB):
                        last = t_.transpose(G[:].bitcast(F16)[:, n * P:(n + 1) * P], w[:, n, :], id16[:])
                    last.then_inc(rows_turned[which].sem, 1)
                elif what == "z":
                    if k == 0:
                        pe.wait_ge(rows1_in.sem, rows1_in.at(b))
                    pe.wait_ge(*read_out)
                    par = parity if k == 0 else 1 - parity
                    last = product(G[:], [(a_w[:, k, s].rearrange("p c d -> p (c d)"), xt1[par][:]) for s in range(2)])
                    last.then_inc(heads_projected.sem, 1)
                elif what == "vo":
                    if k == 0:
                        pe.wait_ge(contexts_in.sem, contexts_in.at(b, PAIRS - 1))
                    pe.wait_ge(*read_out)
                    for p in range(PAIRS):
                        last = product(G[:, p * P:(p + 1) * P], [(context[:, p, blk], vo_w[:, p, :])])
                    last.then_inc(attended.sem, 1)
                elif what == "hid":
                    if k == 0:
                        pe.wait_ge(rows2_in.sem, rows2_in.at(b))
                    pe.wait_ge(*read_out)
                    last = product(G[:], stacked(k * P, (k + 1) * P, xt2[:]))
                    last.then_inc(hidden_ready.sem, 1)
                elif what == "gate":
                    pe.wait_ge(hidden_in.sem, hidden_in.at(b, HB - 1))
                    pe.wait_ge(*read_out)
                    t_.matmul(G[:, 0:NB * E0], ones_rows[:], bias_rows[:, R_G:R_L], start=True, stop=False,
                              skip_group_check=True)
                    for n in range(NB):
                        last = product(G[:, n * E0:(n + 1) * E0],
                                       [(hid[:, m, n * P:(n + 1) * P], wg_w[:, m, :]) for m in range(HB)], start=False)
                    last.then_inc(gate_logits.sem, 1)
                elif what == "y":
                    pe.wait_ge(*read_out)
                    last = product(G[:], [(ones_rows[:], bias_rows[:, R_D:R_3])]
                                   + [(hid[:, m, blk], wd_w[:, m, :]) for m in range(HB)])
                    last.then_inc(experts0_ready.sem, 1)
                elif what == "zl":
                    pe.wait_ge(rows3_in.sem, rows3_in.at(b))
                    pe.wait_ge(*read_out)
                    last = product(G[:], [(z_w[:, s].rearrange("p c d -> p (c d)"), xt3[:]) for s in range(2)])
                    last.then_inc(late_projected.sem, 1)
                elif what == "vl":
                    pe.wait_ge(*read_out)
                    for n in range(NB):
                        last = product(G[:, n * D:(n + 1) * D], stacked(W_V, W_R, xt3[:, n * P:(n + 1) * P], lhs=False))
                    last.then_inc(values_ready.sem, 1)
                elif what == "lg":
                    if k == 0:
                        pe.wait_ge(late_lo_in.sem, late_lo_in.at(b))
                    pe.wait_ge(*read_out)
                    last = product(G[:, 0:512 - k * P], [(xt3[:, blk], zl_t[:, s, k * P:512]) for s in range(2)])
                    last.then_inc(logits_ready.sem, 1)
                elif what == "av":
                    pe.wait_ge(logits_in.sem, logits_in.at(b, NB - 1))
                    pe.wait_ge(values_in.sem, values_in.at(b))
                    pe.wait_ge(*read_out)
                    for n in range(NB):
                        last = product(G[:, n * D:(n + 1) * D],
                                       [(att_t[:, j, n * P:(n + 1) * P], v_l[:, j, :]) for j in range(n + 1)])
                    last.then_inc(late_contexts.sem, 1)
                elif what == "rh":
                    pe.wait_ge(rows4_in.sem, rows4_in.at(b))
                    pe.wait_ge(*read_out)
                    last = product(G[0:RH, :], stacked(W_R, W_E, xt4[:]))
                    last.then_inc(router_hidden.sem, 1)
                elif what == "rl":
                    pe.wait_ge(router_hidden_in.sem, router_hidden_in.at(b))
                    pe.wait_ge(*read_out)
                    t_.matmul(G[:, 0:NB * E1], ones_rows[:], bias_rows[:, R_L:R_ALL], start=True, stop=False,
                              skip_group_check=True)
                    for n in range(NB):
                        last = product(G[:, n * E1:(n + 1) * E1], [(r_hid[:, n * P:(n + 1) * P], rw2_w[:])], start=False)
                    last.then_inc(router_logits.sem, 1)
                elif what == "e1":
                    pe.wait_ge(*read_out)
                    last = product(G[:], stacked(W_E + k * P, W_E + (k + 1) * P, xt4[:]))
                    last.then_inc(layer1_ready.sem, 1)
                elif what == "e2":
                    pe.wait_ge(layer1_in.sem, layer1_in.at(b, k))
                    pe.wait_ge(*read_out)
                    last = product(G[:], [(e2_w[:, k, :], e1_t[:, k, :])])
                    last.then_inc(layer2_ready.sem, 1)
                elif what == "o":
                    if k == 0:
                        pe.wait_ge(layer2_in.sem, layer2_in.at(b, EP - 1))
                    pe.wait_ge(*read_out)
                    t_.matmul(G[:, 0:E1 * D], ones_rows[:], bias_rows[:, R_3:R_G], start=True, stop=False,
                              skip_group_check=True)
                    for p in range(EP):
                        last = product(G[:, p * P:(p + 1) * P], [(e2_t[:, p, blk], e3_w[:, p, :])], start=False)
                    last.then_inc(experts1_ready.sem, 1)

            def scores(b, par, n):
                h, t = n // NB, n % NB
                if t == 0:
                    pe.wait_ge(heads_lo_in.sem, heads_lo_in.at(b, h))
                past, which_k = probs_ready.before(b, n, {0: 2, 1: 2, 2: 5}.get(n, 3))
                if begun(past):
                    pe.wait_ge(probs_ready.sem, probs_ready.at(past, which_k))
                product(s_bank[n % 3][:, 0:T], [(z_t[h % 2][:, s, t * P:(t + 1) * P], xt1[par][:, 0:T]) for s in range(2)])\
                    .then_inc(scores_ready.sem, 1)

            def transpose_probs(b, m):
                pe.wait_ge(probs_ready.sem, probs_ready.at(b, m))
                past, which_k = probs_turned_in.before(b, m, 2)
                if begun(past):
                    pe.wait_ge(probs_turned_in.sem, probs_turned_in.at(past, which_k))
                for j in range(NB):
                    last = t_.transpose(t_bank[m % 2][:, j * P:(j + 1) * P], probs[m % 4][:, j * P:(j + 1) * P], id32[:])
                last.then_inc(probs_turned.sem, 1)

            def contexts(b, par, p, j):
                if j == 0:
                    pe.wait_ge(probs_turned_in.sem, probs_turned_in.at(b, 2 * NB * p + 2 * NB - 1))
                    past, which_k = contexts_in.before(b, p, 1)
                    if begun(past):
                        pe.wait_ge(contexts_in.sem, contexts_in.at(past, which_k))
                for s in range(2):
                    last = t_.matmul(c_bank[s * D:(s + 1) * D, :], xn1[par][:, j, :], probs_t[p % 2][:, s, j, :],
                                     start=j == 0, stop=j == NB - 1, skip_group_check=True)
                if j == NB - 1:
                    last.then_inc(contexts_ready.sem, 1)

            def body(i, parity):
                for n in range(SLOTS):
                    mine = turns_of(n)
                    before, after = mine[:1], mine[1:]
                    for x_ in before:
                        if active(i, x_[1]):
                            turn(i, parity, *x_)
                    if active(i, "attn"):
                        scores(i - 1, 1 - parity, n)
                    for x_ in after:
                        if active(i, x_[1]):
                            turn(i, parity, *x_)
                    if n >= 3 and active(i, "attn"):
                        transpose_probs(i - 1, n - 3)
                    if n < 3 and active(i, "mid"):
                        transpose_probs(i - 2, SLOTS + n - 3)
                    p, j = divmod(n - 11, 8)
                    if n >= 11 and j < NB and active(i, "attn"):
                        contexts(i - 1, 1 - parity, p, j)
                    if 3 <= n < 3 + NB and active(i, "mid"):
                        contexts(i - 2, parity, PAIRS - 1, n - 3)

            each_iteration(pe, body)


_INS = ['x', 'L0_tok_kernel', 'L0_tok_bias', 'L0_tok_beta', 'L0_tok_moving_mean', 'L0_tok_moving_var',
        'L0_attn_Q', 'L0_attn_K', 'L0_attn_VO', 'L0_ffn_W1', 'L0_ffn_b1', 'L0_ffn_Wg', 'L0_ffn_bg',
        'L0_ffn_Wd', 'L0_ffn_bd', 'L1_attn_Wq', 'L1_attn_Wk', 'L1_attn_Wv', 'L1_attn_Wo',
        'L1_ffn_router_w1', 'L1_ffn_router_b1', 'L1_ffn_router_w2', 'L1_ffn_router_b2',
        'L1_ffn_expert_w1', 'L1_ffn_expert_b1', 'L1_ffn_expert_w2', 'L1_ffn_expert_b2',
        'L1_ffn_expert_w3', 'L1_ffn_expert_b3']


def kernel(**inputs):
    import numpy as _np
    import concourse.bacc as _bacc
    from concourse import mybir as _mybir
    from concourse.bass_utils import run_bass_kernel_spmd as _run

    nc = _bacc.Bacc("TRN2", target_bir_lowering=False, num_devices=1)
    arrays, args = {}, []
    for name in _INS:
        a = _np.ascontiguousarray(inputs[name])
        arrays[f"in_{name}"] = a
        args.append(nc.dram_tensor(f"in_{name}", a.shape, _mybir.dt.from_np(a.dtype), kind="ExternalInput").ap())
    args.append(nc.dram_tensor("out_0", (B, T, D), F32, kind="ExternalOutput").ap())
    tower(nc, *args)
    r = _run(nc, [arrays], core_ids=[0])
    return r.results[0]["out_0"]
```

```python
import concourse.bass as bass
import concourse.mybir as mybir
from contextlib import ExitStack

F32 = mybir.dt.float32
F16 = mybir.dt.float16
BF16 = mybir.dt.bfloat16
I32 = mybir.dt.int32
ALU = mybir.AluOpType
ACT = mybir.ActivationFunctionType
AX = mybir.AxisListType.X

P = 128
B, T_IN, C_IN = 32, 512, 128
TAPS, D = 3, 64
T = T_IN - TAPS + 1
NB = T_IN // P
H0, R0 = 8, 32
PAIRS = H0 // 2
HID, E0 = 256, 8
HB = HID // P
E1, RH = 6, 32
EP = E1 // 2
SLOTS = H0 * NB
TAIL = T - (NB - 1) * P

XS, WS = 64.0, 256.0
ZS = 1.0 / 128.0
ONE = 512.0
LIN = XS * WS
LOGIT = LIN * ZS * XS
LN_EPS, BN_EPS = 1e-5, 1e-3
TINY = 1e-30

W_HID, W_Z, W_V, W_R, W_E = 0, HID, HID + D, HID + 2 * D, HID + 2 * D + RH
W_ALL = W_E + E1 * D
SEGMENTS = [(W_HID, W_Z), (W_Z, W_V), (W_V, W_R), (W_R, W_E), (W_E, W_ALL)]
SG_HID, SG_Z, SG_V, SG_R, SG_E = range(H0, H0 + 5)
N_SG = H0 + 5
R_D, R_3, R_G, R_L = 0, E0 * D, E0 * D + E1 * D, E0 * D + E1 * D + NB * E0
R_ALL = R_L + NB * E1

LAG = {"front": 0, "attn": 1, "mid": 2, "late": 3}
STEPS = B + max(LAG.values())

TURNS = [
    (2, "late", "zl", 0), (2, "attn", "z", 4), (2, "late", "vl", 0),
    (3, "late", "lg", 0), (3, "late", "lg", 1),
    (5, "late", "lg", 2), (5, "late", "lg", 3), (5, "mid", "sums", 0), (5, "attn", "shift", 1),
    (5, "mid", "vo", 0),
    (6, "mid", "vo", 1),
    (7, "attn", "z", 5), (7, "mid", "vo", 2),
    (8, "mid", "vo", 3), (8, "late", "av", 0),
    (10, "attn", "z", 6),
    (11, "front", "xq", 0),
    (12, "front", "conv", 0),
    (14, "mid", "xt2", 0), (14, "attn", "shift", 2), (14, "mid", "hid", 0),
    (15, "mid", "hid", 1), (15, "attn", "z", 7), (15, "mid", "gate", 0),
    (17, "late", "xt4", 0), (17, "late", "rh", 0), (17, "late", "e1", 0), (17, "late", "e1", 1),
    (18, "front", "xt1", 0),
    (19, "late", "rl", 0),
    (20, "front", "z", 0), (20, "front", "z", 1),
    (21, "attn", "shift", 3), (21, "late", "e1", 2),
    (22, "late", "e2", 0), (22, "late", "e2", 1),
    (23, "mid", "y", 0),
    (24, "mid", "y", 1),
    (25, "mid", "y", 2),
    (26, "mid", "y", 3), (26, "late", "e2", 2),
    (27, "late", "o", 0),
    (28, "front", "z", 2), (28, "late", "o", 1), (28, "front", "shift", 0),
    (29, "late", "o", 2),
    (30, "front", "z", 3),
    (31, "late", "o", 3), (31, "mid", "xt3", 0),
]
STEP_AT = {
    "signs": 4,
    "centre1": 13, "var1": 14, "factor1": 14, "parts1": 15,
    "centre2": 9, "var2": 9, "factor2": 10, "parts2": 11,
    "gate_exp": 17, "gate": 20,
    "centre3": 27, "var3": 27, "factor3": 28, "parts3": 29,
    "centre4": 12, "var4": 12, "factor4": 12, "parts4": 14,
    "router_exp": 19, "route": 19, "second": 21, "second_exp": 22, "route_end": 23,
    "store_context": 3,
}
G_BANKS, M_BANKS, C_BANKS = 3, 2, 1
M_AHEAD = 12
C_LAG = 4
BEFORE_SCORES = [0, 0, 1, 1, 0, 0, 1, 1, 2, 0, 1, 1, 1, 0, 1, 2, 0, 1, 0, 1, 2, 1, 1, 1, 0, 1, 2, 1, 1, 1, 1, 1]
BEFORE_MAXIMA = [0, 0, 2, 2, 0, 2, 1, 2, 2, 0, 1, 1, 1, 0, 2, 2, 0, 1, 1, 1, 2, 2, 2, 1, 1, 1, 2, 1, 2, 1, 1, 2]
BEFORE_EXP = [0, 0, 1, 1, 0, 0, 1, 0, 1, 0, 0, 1, 1, 0, 0, 1, 0, 1, 1, 1, 1, 1, 1, 1, 1, 1, 2, 1, 1, 0, 1, 1]
BEFORE_MAX = [0, 0, 1, 2, 0, 2, 1, 1, 2, 0, 1, 0, 0, 0, 1, 2, 0, 2, 1, 1, 2, 1, 2, 1, 1, 1, 2, 1, 2, 0, 0, 2]
VO_SLOTS = [slot for slot, _, what, _ in TURNS if what == "vo"]
Y_SLOTS = [slot for slot, _, what, _ in TURNS if what == "y"]
O_SLOTS = [slot for slot, _, what, _ in TURNS if what == "o"]


def begun(b):
    return not isinstance(b, int) or b >= 0


def last_scores(h):
    return 2 * NB * (h // 2) + 2 * (NB - 1) + h % 2


class Signal:

    def __init__(self, sem, per, unit=1):
        self.sem, self.per, self.unit = sem, per, unit

    def at(self, b, k=0):
        return b * (self.per * self.unit) + (k + 1) * self.unit

    def before(self, b, k, back):
        k -= back
        while k < 0:
            b, k = b - 1, k + self.per
        return b, k


class Chain:

    def __init__(self, sem, per):
        self.sem, self.per, self.n = sem, per, 0

    def link(self, eng, b, ins):
        ins.then_inc(self.sem, 1)
        self.n += 1
        eng.wait_ge(self.sem, b * self.per + self.n)

    def end(self):
        assert self.n == self.per, (self.n, self.per)
        self.n = 0


def tower(nc, x, kern, bias, beta, mean, var, Q, K, VO, W1, b1, Wg, bg, Wd, bd, Wq, Wk, Wv, Wo,
          rw1, rb1, rw2, rb2, ew1, eb1, ew2, eb2, ew3, eb3, out):
    ctx = ExitStack()
    with ctx:
        def sb(name, shape, dt=F32):
            return ctx.enter_context(nc.sbuf_tensor(name, shape, dt))

        def ps(name):
            return ctx.enter_context(nc.psum_tensor(name, [P, 512], F32))

        def sem(name):
            return ctx.enter_context(nc.semaphore(name))

        def signal(name, per=1, unit=1):
            return Signal(sem(name), per, unit)

        q_dup = sb("q_dup", [R0, H0, 2, D])
        k_raw = sb("k_raw", [R0, H0, D])
        q_first = sb("q_first", [R0, H0, 2, 1])
        k_first = sb("k_first", [R0, H0, 1])
        wq_dup = sb("wq_dup", [D, 2, D])
        wv_dup = sb("wv_dup", [D, 2, D])
        wk_raw = sb("wk_raw", [D, D])
        wo_raw = sb("wo_raw", [D, D])
        wo_t = sb("wo_t", [D, D])
        w_raw = sb("w_raw", [P, W_ALL])
        w_nrm = sb("w_nrm", [P, W_ALL])
        a_nrm = sb("a_nrm", [P, H0, D])
        w_hi = sb("w_hi", [P, W_ALL], F16)
        w_lo = sb("w_lo", [P, W_ALL], F16)
        a_w = sb("a_w", [P, H0, 2, 2, D], F16)
        z_w = sb("z_w", [P, 2, 2, D], F16)
        amax = sb("amax", [P, N_SG])
        sigma = sb("sigma", [P, N_SG])
        rsigma = sb("rsigma", [P, N_SG])
        exp_scale = sb("exp_scale", [P, H0])
        hid_scale = sb("hid_scale", [P, 1])
        unscale = sb("unscale", [P, N_SG])
        rescale = sb("rescale", [P, N_SG])
        vo_w = sb("vo_w", [P, PAIRS, P])
        wd_w = sb("wd_w", [P, HB, E0 * D])
        wg_w = sb("wg_w", [P, HB, E0])
        b1_c = sb("b1_c", [P, HB])
        rw2_w = sb("rw2_w", [RH, E1])
        rb1_c = sb("rb1_c", [RH, 1])
        e2_w = sb("e2_w", [P, EP, P])
        e3_w = sb("e3_w", [P, EP, P])
        eb1_c = sb("eb1_c", [P, EP])
        eb2_c = sb("eb2_c", [P, EP])
        row = sb("row", [1, R_ALL])
        row_rest = sb("row_rest", [1, 2, R_ALL])
        row_part = sb("row_part", [1, 3, R_ALL], BF16)
        bias_rows = sb("bias_rows", [3, R_ALL], BF16)
        ones_rows = sb("ones_rows", [3, P], BF16)
        k_raw0 = sb("k_raw0", [P, TAPS, D])
        k_sign = sb("k_sign", [P, TAPS, D], BF16)
        bn_raw = sb("bn_raw", [P, 4, D])
        bn_inv = sb("bn_inv", [P, D])
        bn_exp = sb("bn_exp", [P, D])
        bn_scale = sb("bn_scale", [P, D])
        bn_shift = sb("bn_shift", [P, D])
        id32 = sb("id32", [P, P])
        ones32 = sb("ones32", [H0, P])
        top = sb("top", [H0, 1])
        peak = sb("peak", [H0, H0])
        id16 = sb("id16", [P, P], F16)
        idb = sb("idb", [P, P], BF16)
        causal = sb("causal", [P, 512])
        row_no = sb("row_no", [P, NB], I32)
        row_scale = sb("row_scale", [P, NB])
        rank_i = sb("rank_i", [P, E0], I32)
        rank = sb("rank", [P, E0])
        minus_half = sb("minus_half", [P, NB])
        per_one = sb("per_one", [P, 2 * NB])
        vo_first = sb("vo_first", [P, PAIRS, D])

        x_in = sb("x_in", [P, NB, C_IN])
        x_sign = sb("x_sign", [P, NB, C_IN], BF16)
        xq_t = sb("xq_t", [P, T_IN + TAPS - 1], BF16)
        h0 = [sb(f"h0_{i}", [P, NB, D]) for i in range(2)]
        ln = []
        for i in range(4):
            ln.append(dict(
                sum=sb(f"ln{i}_sum", [P, NB]), mu=sb(f"ln{i}_mu", [P, NB]),
                d=sb(f"ln{i}_d", [P, NB, D]), sq=sb(f"ln{i}_sq", [P, NB, D]),
                sum2=sb(f"ln{i}_sum2", [P, NB]), var=sb(f"ln{i}_var", [P, NB]),
                r=sb(f"ln{i}_r", [P, NB]), parts=sb(f"ln{i}_parts", [P, NB, 2 * D], F16)))
        xn1 = [sb(f"xn1_{i}", [P, NB, D]) for i in range(2)]
        xn_other = [sb(f"xn_{i}", [P, NB, D]) for i in (2, 3, 4)]
        xt1 = [sb(f"xt1_{i}", [P, 512], F16) for i in range(2)]
        xt2, xt3, xt4 = (sb(f"xt{i}", [P, 512], F16) for i in (2, 3, 4))
        z_all = sb("z_all", [P, H0, 2, 512], F16)
        z_t = [z_all[:, h] for h in range(H0)]
        z_whole = [sb(f"z_whole{i}", [P, 512]) for i in range(2)]
        neg_max = sb("neg_max", [P, SLOTS])
        shift = sb("shift", [P, SLOTS], F16)
        shift_rows = sb("shift_rows", [2 * NB, P], F16)
        probs = [sb(f"probs{i}", [P, 512]) for i in range(8)]
        context = sb("context", [P, PAIRS, 512])
        sum_rows = sb("sum_rows", [H0, 512])
        row_inv = sb("row_inv", [P, SLOTS])
        vo_tmp = [sb(f"vo_tmp{i}", [P, H0, D]) for i in range(2)]
        h1 = sb("h1", [P, NB, D])
        hid = sb("hid", [P, HB, 512])
        g_max, g_sum, g_inv, g_top = (sb(n, [P, NB]) for n in ("g_max", "g_sum", "g_inv", "g_top"))
        g_off, g_exp, g_key, g_hot, gate = (
            sb(n, [P, NB, E0]) for n in ("g_off", "g_exp", "g_key", "g_hot", "gate"))
        y_tmp = [sb(f"y_tmp{i}", [P, E0, D]) for i in range(2)]
        h2 = sb("h2", [P, NB, D])
        zl_t = sb("zl_t", [P, 2, 512], F16)
        v_l = sb("v_l", [P, NB, D])
        att_t = sb("att_t", [P, NB, 512])
        av_tmp = sb("av_tmp", [P, NB, D])
        h3 = sb("h3", [P, NB, D])
        r_hid = sb("r_hid", [RH, 512])
        r_max, r_sum, r_inv, r_top, r_top2, r_second, r_gap, r_e2, r_den, r_w1, r_w2 = (
            sb(n, [P, NB]) for n in ("r_max", "r_sum", "r_inv", "r_top", "r_top2", "r_second",
                                     "r_gap", "r_e2", "r_den", "r_w1", "r_w2"))
        r_off, r_exp, r_p, r_key, r_hot, r_rest, r_is2, r_key2, r_hot2, r_g1, r_g2, r_gate = (
            sb(n, [P, NB, E1]) for n in ("r_off", "r_exp", "r_p", "r_key", "r_hot", "r_rest", "r_is2",
                                         "r_key2", "r_hot2", "r_g1", "r_g2", "r_gate"))
        e1_t = sb("e1_t", [P, EP, 512])
        e2_t = sb("e2_t", [P, EP, 512])
        o_tmp = [sb(f"o_tmp{i}", [P, E1, D]) for i in range(2)]
        out_sb = sb("out_sb", [P, NB, D])

        s_bank = [ps(f"s_bank{i}") for i in range(2)]
        m_bank = [ps(f"m_bank{i}") for i in range(M_BANKS)]
        c_bank = [ps(f"c_bank{i}") for i in range(C_BANKS)]
        g_bank = [ps(f"g_bank{i}") for i in range(G_BANKS)]

        zeroed = sem("zeroed")
        front_weights_in = sem("front_weights_in")
        weights_in = sem("weights_in")
        consts_made = sem("consts_made")
        pool_setup = sem("pool_setup")
        dve_setup = sem("dve_setup")
        first_off = sem("first_off")
        heads_folded = sem("heads_folded")
        folded = sem("folded")
        wo_ready = sem("wo_ready")
        amax_ready = sem("amax_ready")
        amax_turned = sem("amax_turned")
        peak_ready = sem("peak_ready")
        sigma_ready = sem("sigma_ready")
        front_ready = sem("front_ready")
        bn_var = sem("bn_var")
        bn_pow = sem("bn_pow")
        rows_split = sem("rows_split")
        rows_in = sem("rows_in")
        ready = sem("ready")

        x_loaded = signal("x_loaded", 1, 16)
        stored = signal("stored", 2, 16)
        sums_moved = signal("sums_moved", PAIRS, 16)
        shift_moved = signal("shift_moved", PAIRS, 2 * 16)
        x_turned = signal("x_turned")
        conv_done = signal("conv_done")
        rows1_turned = signal("rows1_turned")
        heads_projected = signal("heads_projected", H0)
        scores_ready = signal("scores_ready", SLOTS)
        shift_turned = signal("shift_turned", PAIRS)
        sums_ready = signal("sums_ready")
        scores_for_max = signal("scores_for_max", SLOTS)
        contexts_ready = signal("contexts_ready", SLOTS // 2)
        attended = signal("attended", NB)
        rows2_turned = signal("rows2_turned")
        hidden_ready = signal("hidden_ready", HB)
        gate_logits = signal("gate_logits")
        experts0_ready = signal("experts0_ready", NB)
        rows3_turned = signal("rows3_turned")
        late_projected = signal("late_projected")
        values_ready = signal("values_ready")
        logits_ready = signal("logits_ready", NB)
        late_contexts = signal("late_contexts")
        rows4_turned = signal("rows4_turned")
        router_hidden = signal("router_hidden")
        router_logits = signal("router_logits")
        layer1_ready = signal("layer1_ready", EP)
        layer2_ready = signal("layer2_ready", EP)
        experts1_ready = signal("experts1_ready", NB)
        x_turned_in = signal("x_turned_in")
        rows1_in = signal("rows1_in")
        heads_hi_in = signal("heads_hi_in", H0)
        heads_whole_in = signal("heads_whole_in", H0)
        probs_ready = signal("probs_ready", SLOTS)
        shift_in = signal("shift_in", PAIRS)
        contexts_in = signal("contexts_in", PAIRS)
        rows2_in = signal("rows2_in")
        hidden_in = signal("hidden_in", HB)
        gate_exp = signal("gate_exp")
        rows3_in = signal("rows3_in")
        late_hi_in = signal("late_hi_in")
        values_in = signal("values_in")
        rows4_in = signal("rows4_in")
        router_hidden_in = signal("router_hidden_in")
        router_exp = signal("router_exp", 2)
        layer1_in = signal("layer1_in", EP)
        layer2_in = signal("layer2_in", EP)
        signs_ready = signal("signs_ready")
        conv_in = signal("conv_in")
        var1_ready = signal("var1_ready")
        var2_ready = signal("var2_ready")
        var3_ready = signal("var3_ready")
        var4_ready = signal("var4_ready")
        parts1_ready = signal("parts1_ready")
        parts2_ready = signal("parts2_ready")
        parts3_ready = signal("parts3_ready")
        parts4_ready = signal("parts4_ready")
        max_ready = signal("max_ready", SLOTS)
        sums_inverted = signal("sums_inverted")
        attended_in = signal("attended_in", NB)
        gate_offsets = signal("gate_offsets")
        gate_ready = signal("gate_ready")
        experts0_in = signal("experts0_in", NB)
        late_lo_in = signal("late_lo_in")
        logits_in = signal("logits_in", NB)
        late_contexts_in = signal("late_contexts_in")
        h3_ready = signal("h3_ready")
        router_offsets = signal("router_offsets")
        gap_ready = signal("gap_ready")
        route_ready = signal("route_ready")
        experts1_in = signal("experts1_in", NB)
        shift_ready = signal("shift_ready", PAIRS)
        heads_lo_in = signal("heads_lo_in", H0)
        factor1_ready = signal("factor1_ready")
        factor2_ready = signal("factor2_ready")
        factor3_ready = signal("factor3_ready")
        factor4_ready = signal("factor4_ready")
        h1_ready = signal("h1_ready", NB)
        h2_ready = signal("h2_ready", NB)
        out_ready = signal("out_ready", NB)
        var_ready = [None, var1_ready, var2_ready, var3_ready, var4_ready]
        parts_ready = [None, parts1_ready, parts2_ready, parts3_ready, parts4_ready]
        factor_ready = [None, factor1_ready, factor2_ready, factor3_ready, factor4_ready]
        rows_turned = [None, rows1_turned, rows2_turned, rows3_turned, rows4_turned]
        ve_front = Chain(sem("ve_front"), 8)
        ve_mid = Chain(sem("ve_mid"), 20)
        ve_late = Chain(sem("ve_late"), 25)
        po_mid = Chain(sem("po_mid"), 3 * NB + 3 * NB)
        po_late = Chain(sem("po_late"), 3 * NB)

        READ_OUT = {
            "xq": x_turned_in, "conv": conv_in, "xt1": rows1_in, "z": heads_whole_in, "shift": shift_in,
            "sums": sums_inverted, "vo": attended_in,
            "xt2": rows2_in, "hid": hidden_in, "gate": gate_offsets, "y": experts0_in,
            "xt3": rows3_in, "zl": late_lo_in, "vl": values_in, "lg": logits_in, "av": late_contexts_in,
            "xt4": rows4_in, "rh": router_hidden_in, "rl": router_offsets, "e1": layer1_in, "e2": layer2_in,
            "o": experts1_in}

        def active(i, stage):
            return not isinstance(i, int) or 0 <= i - LAG[stage] < B

        def last_use(i, at):
            j, p = i, at
            while True:
                p -= 1
                if p < 0:
                    j, p = j - 1, p + len(TURNS)
                if isinstance(j, int) and j < 0:
                    return consts_made, 1
                _, stage, what, k = TURNS[p]
                if p % G_BANKS == at % G_BANKS and active(j, stage):
                    read = READ_OUT[what]
                    return read.sem, read.at(j - LAG[stage], k)

        def turns_of(n):
            return [(at, stage, what, k) for at, (slot, stage, what, k) in enumerate(TURNS) if slot == n]

        def each_iteration(eng, body, after_first=None, after_second=None):
            first = max(LAG.values()) + 1
            for i in range(first):
                body(i, i % 2)
                if i == 0 and after_first:
                    after_first()
                if i == 1 and after_second:
                    after_second()
            with eng.Fori(first // 2, B // 2) as two:
                body(two * 2, 0)
                body(two * 2 + 1, 1)
            for i in range(B, STEPS):
                body(i, i % 2)

        FRONT_LOADS = 8
        MORE_LOADS, ACT_LOADS = 12 + 4, HB + 4 + 12
        block = ctx.enter_context(nc.Block())

        @block.sync
        def _(sp):
            def load(dst, src):
                nonlocal n
                sp.dma_start(dst, src).then_inc(arrived, 16)
                n += 1

            n, arrived = 0, front_weights_in
            with nc.allow_non_contiguous_dma(reason="weights, once"):
                for c in range(2):
                    load(q_dup[:, :, c, :], Q.rearrange("h r d -> r h d"))
                load(k_raw[:], K.rearrange("h r d -> r h d"))
                load(k_raw0[:], kern.rearrange("k c o -> c k o"))
                for i, v in enumerate((bias, mean, var, beta)):
                    load(bn_raw[:, i, :], v.partition_broadcast(P))
            assert n == FRONT_LOADS, n

            def load_rest():
                nonlocal n, arrived
                n, arrived = 0, weights_in
                with nc.allow_non_contiguous_dma(reason="weights, once"):
                    load(wo_raw[:], Wo)
                    load(wk_raw[:], Wk)
                    for c in range(2):
                        load(wq_dup[:, c, :], Wq)
                        load(wv_dup[:, c, :], Wv)
                        half = w_raw[D * c:D * c + D, :]
                        load(half[:, W_HID:W_Z], W1)
                        load(half[:, W_R:W_E], rw1)
                        load(half[:, W_E:W_ALL].rearrange("d (e h) -> d e h", e=E1),
                             ew1.rearrange("e d h -> d e h"))
                    load(row[:, R_D:R_3], bd.rearrange("(o e) c -> o (e c)", o=1))
                    load(row[:, R_3:R_G], eb3.rearrange("(o e) c -> o (e c)", o=1))
                    load(row[:, R_G:R_L].rearrange("o (t e) -> o t e", t=NB), bg.partition_broadcast(NB))
                    load(row[:, R_L:R_ALL].rearrange("o (t e) -> o t e", t=NB), rb2.partition_broadcast(NB))
                assert n == MORE_LOADS, n

            def move_rows():
                sp.wait_ge(rows_split, 1)
                for r in range(3):
                    sp.dma_start(bias_rows[r:r + 1, :], row_part[:, r, :]).then_inc(rows_in, 16)

            def load_x(b):
                if begun(b - 1):
                    sp.wait_ge(signs_ready.sem, signs_ready.at(b - 1))
                sp.dma_start(x_in[:], x[b].rearrange("(n p) c -> p n c", p=P)).then_inc(x_loaded.sem, 16)

            def body(i, parity):
                def move_sums(b, p):
                    sp.wait_ge(contexts_in.sem, contexts_in.at(b, p))
                    if begun(b - 1):
                        sp.wait_ge(sums_ready.sem, sums_ready.at(b - 1))
                    sp.dma_start(sum_rows[2 * p:2 * p + 2, :], context[0:D + 1:D, p, :]).then_inc(sums_moved.sem, 16)

                def move_shift(b, p):
                    sp.wait_ge(shift_in.sem, shift_in.at(b, p))
                    for s in range(2):
                        sp.dma_start(z_all[0:1, 2 * p + s, 0, :].rearrange("o (n q) -> o n q", n=NB),
                                     shift_rows[NB * s:NB * (s + 1), :]).then_inc(shift_moved.sem, 16)

                if active(i, "front") and begun(i - 1):
                    load_x(i)
                if active(i, "mid"):
                    move_sums(i - LAG["mid"], PAIRS - 1)
                if active(i, "attn"):
                    for p in range(PAIRS - 1):
                        move_shift(i - LAG["attn"], p + 1)
                        move_sums(i - LAG["attn"], p)
                if active(i, "front"):
                    move_shift(i, 0)
                if active(i, "late"):
                    b = i - LAG["late"]
                    sp.wait_ge(out_ready.sem, out_ready.at(b, NB - 1))
                    sp.dma_start(out[b, 0:T - TAIL, :].rearrange("(n p) c -> p n c", p=P),
                                 out_sb[:, 0:NB - 1, :]).then_inc(stored.sem, 16)
                    sp.dma_start(out[b, T - TAIL:T, :], out_sb[0:TAIL, NB - 1, :]).then_inc(stored.sem, 16)

            load_x(0)
            load_rest()
            each_iteration(sp, body, after_first=move_rows)
            sp.wait_ge(stored.sem, stored.at(B - 1, 1))

        @block.gpsimd
        def _(pool):
            g = nc.gpsimd
            n = 0

            def link(ins):
                nonlocal n
                ins.then_inc(pool_setup, 1)
                n += 1
                pool.wait_ge(pool_setup, n)

            for t in (id32, id16, idb):
                link(g.memset(t[:], 0.0))
                link(g.affine_select(out=t[:], in_=t[:], compare_op=ALU.not_equal, fill=1.0, base=0,
                                     pattern=[[-1, P]], channel_multiplier=1))
            link(g.memset(minus_half[:], -0.5))
            link(g.memset(bn_exp[:], -0.5))
            link(g.memset(ones32[:], 1.0))
            link(g.memset(xq_t[:, T_IN:], 0.0))
            link(g.memset(per_one[:], 1.0 / ONE))
            for t in xn1:
                link(g.memset(t[:, :, 0:1], 1.0))
            link(g.memset(ln[0]["parts"][:, :, 0:1], ONE))
            link(g.memset(ln[0]["parts"][:, :, D:D + 1], 0.0))
            g.memset(xq_t[:, 0:T_IN], 0.0).then_inc(consts_made, 1)
            for t in (vo_w, e2_w, e3_w):
                g.memset(t[:], 0.0).then_inc(zeroed, 1)
            pool.wait_ge(bn_var, 1)
            g.tensor_tensor(bn_inv[:], bn_raw[:, 2, :], bn_exp[:], ALU.pow).then_inc(bn_pow, 1)
            link(g.memset(causal[:], 1.0))
            link(g.affine_select(out=causal[:], in_=causal[:], compare_op=ALU.is_ge, fill=0.0, base=0,
                                 pattern=[[1, 512]], channel_multiplier=-1))
            link(g.iota(row_no[:], pattern=[[P, NB]], base=0, channel_multiplier=1))
            link(g.iota(rank_i[:], pattern=[[-1, E0]], base=E0, channel_multiplier=0))
            g.memset(ones_rows[:], 1.0).then_inc(consts_made, 1)

            def inverse_root(stage, i, b):
                pool.wait_ge(var_ready[stage].sem, var_ready[stage].at(b))
                g.tensor_tensor(ln[stage - 1]["r"][:], ln[stage - 1]["var"][:], minus_half[:],
                                ALU.pow).then_inc(factor_ready[stage].sem, 1)

            def tree(chain, b, t, n_parts, last_in, last_out, last_sem):
                if n_parts == 8:
                    chain.link(pool, b, g.tensor_tensor(t[:, 0:4], t[:, 0:4], t[:, 4:8], ALU.add))
                    chain.link(pool, b, g.tensor_tensor(t[:, 0:2], t[:, 0:2], t[:, 2:4], ALU.add))
                else:
                    chain.link(pool, b, g.tensor_tensor(t[:, 0:3], t[:, 0:3], t[:, 3:6], ALU.add))
                    chain.link(pool, b, g.tensor_tensor(t[:, 1], t[:, 1], t[:, 2], ALU.add))
                chain.link(pool, b, g.tensor_tensor(t[:, 0], t[:, 0], t[:, 1], ALU.add))
                g.tensor_tensor(last_out, t[:, 0], last_in, ALU.add).then_inc(last_sem, 1)

            def body(i, parity):
                for n in range(SLOTS):
                    for _, stage, what, k in turns_of(n):
                        if what == "z" and active(i, stage):
                            b = i - LAG[stage]
                            pool.wait_ge(heads_whole_in.sem, heads_whole_in.at(b, k))
                            if begun(b - 1):
                                pool.wait_ge(scores_ready.sem, scores_ready.at(b - 1, last_scores(k)))
                            g.tensor_tensor(z_t[k][:, 1, :], z_whole[k % 2][:], z_t[k][:, 0, :],
                                            ALU.subtract).then_inc(heads_lo_in.sem, 1)
                    p, t = divmod(n + M_AHEAD, 2 * NB)
                    if t == 2 * NB - 1:
                        b = i if p >= PAIRS else i - LAG["attn"]
                        p %= PAIRS
                        if active(i, "attn" if b is not i else "front"):
                            pair = slice(2 * NB * p, 2 * NB * (p + 1))
                            pool.wait_ge(max_ready.sem, max_ready.at(b, pair.stop - 1))
                            g.tensor_tensor(shift[:, pair], neg_max[:, pair], per_one[:],
                                            ALU.mult).then_inc(shift_ready.sem, 1)
                    if active(i, "mid"):
                        b = i - LAG["mid"]
                        if n in VO_SLOTS:
                            t = VO_SLOTS.index(n)
                            pool.wait_ge(attended_in.sem, attended_in.at(b, t))
                            tree(po_mid, b, vo_tmp[t % 2], 8, h0[parity][:, t], h1[:, t], h1_ready.sem)
                        if n in Y_SLOTS:
                            t = Y_SLOTS.index(n)
                            pool.wait_ge(experts0_in.sem, experts0_in.at(b, t))
                            if t == 0:
                                if begun(b - 1):
                                    pool.wait_ge(h3_ready.sem, h3_ready.at(b - 1))
                            tree(po_mid, b, y_tmp[t % 2], 8, h1[:, t], h2[:, t], h2_ready.sem)
                        if n == STEP_AT["factor2"]:
                            inverse_root(2, i, b)
                        if n == STEP_AT["factor3"]:
                            inverse_root(3, i, b)
                    if active(i, "late"):
                        b = i - LAG["late"]
                        if n == STEP_AT["factor4"]:
                            inverse_root(4, i, b)
                        if n in O_SLOTS:
                            t = O_SLOTS.index(n)
                            pool.wait_ge(experts1_in.sem, experts1_in.at(b, t))
                            if t == 0:
                                if begun(b - 1):
                                    pool.wait_ge(stored.sem, stored.at(b - 1, 1))
                            tree(po_late, b, o_tmp[t % 2], 6, h3[:, t], out_sb[:, t], out_ready.sem)
                    if active(i, "front") and n == STEP_AT["factor1"]:
                        inverse_root(1, i, i)
                if active(i, "mid"):
                    po_mid.end()
                if active(i, "late"):
                    po_late.end()

            each_iteration(pool, body)

        @block.scalar
        def _(act):
            a = nc.scalar
            n = 0

            def load(dst, src):
                nonlocal n
                act.dma_start(dst, src).then_inc(weights_in, 16)
                n += 1

            with nc.allow_non_contiguous_dma(reason="weights, once"):
                for m in range(HB):
                    load(wd_w[:, m, :].rearrange("j (e c) -> j e c", e=E0),
                         Wd[:, m * P:(m + 1) * P, :].rearrange("e j c -> j e c"))
                load(wg_w[:], Wg.rearrange("(m j) e -> j m e", m=HB))
                load(b1_c[:], b1.rearrange("(m j) -> j m", m=HB))
                load(rw2_w[:], rw2)
                load(rb1_c[:], rb1.rearrange("(r o) -> r o", o=1))
                act.wait_ge(zeroed, 3)
                for c in range(2):
                    half = slice(D * c, D * c + D)
                    load(vo_w[half, :, half], VO.rearrange("(p s) d e -> s d p e", s=2)[c])
                    load(vo_first[half, :, :], VO.rearrange("(p s) d e -> s d p e", s=2)[c, 0].partition_broadcast(D))
                    load(e2_w[half, :, half], ew2.rearrange("(p s) d e -> s d p e", s=2)[c])
                    load(e3_w[half, :, half], ew3.rearrange("(p s) d e -> s d p e", s=2)[c])
                    load(eb1_c[half, :], eb1.rearrange("(p s) h -> s h p", s=2)[c])
                    load(eb2_c[half, :], eb2.rearrange("(p s) h -> s h p", s=2)[c])
            assert n == ACT_LOADS, n
            act.wait_ge(front_ready, 1)

            def store_turn(i, parity, at, stage, what, k):
                b = i - LAG[stage]
                G = g_bank[at % G_BANKS]
                if what == "xq":
                    act.wait_ge(x_turned.sem, x_turned.at(b))
                    if begun(b - 1):
                        act.wait_ge(conv_done.sem, conv_done.at(b - 1))
                    a.activation(xq_t[:, 0:T_IN], G[:].bitcast(BF16)[:, 0:T_IN], ACT.Copy).then_inc(x_turned_in.sem, 1)
                elif what == "xt1":
                    act.wait_ge(rows1_turned.sem, rows1_turned.at(b))
                    if begun(b - 2):
                        act.wait_ge(scores_ready.sem, scores_ready.at(b - 2, SLOTS - 1))
                    a.activation(xt1[parity][:], G[:].bitcast(F16)[:, 0:512], ACT.Copy).then_inc(rows1_in.sem, 1)
                elif what == "xt2":
                    act.wait_ge(rows2_turned.sem, rows2_turned.at(b))
                    if begun(b - 1):
                        act.wait_ge(hidden_ready.sem, hidden_ready.at(b - 1, HB - 1))
                    a.activation(xt2[:], G[:].bitcast(F16)[:, 0:512], ACT.Copy).then_inc(rows2_in.sem, 1)
                elif what == "xt3":
                    act.wait_ge(rows3_turned.sem, rows3_turned.at(b))
                    if begun(b - 1):
                        act.wait_ge(logits_ready.sem, logits_ready.at(b - 1, NB - 1))
                    a.activation(xt3[:], G[:].bitcast(F16)[:, 0:512], ACT.Copy).then_inc(rows3_in.sem, 1)
                elif what == "xt4":
                    act.wait_ge(rows4_turned.sem, rows4_turned.at(b))
                    if begun(b - 1):
                        act.wait_ge(layer1_ready.sem, layer1_ready.at(b - 1, EP - 1))
                    a.activation(xt4[:], G[:].bitcast(F16)[:, 0:512], ACT.Copy).then_inc(rows4_in.sem, 1)
                elif what == "z":
                    act.wait_ge(heads_projected.sem, heads_projected.at(b, k))
                    if begun(b - 1):
                        act.wait_ge(scores_ready.sem, scores_ready.at(b - 1, last_scores(k)))
                    a.activation(z_t[k][:, 0, :], G[:], ACT.Copy, scale=ZS).then_inc(heads_hi_in.sem, 1)
                    past, which_k = heads_lo_in.before(b, k, 2)
                    if begun(past):
                        act.wait_ge(heads_lo_in.sem, heads_lo_in.at(past, which_k))
                    a.activation(z_whole[k % 2][:], G[:], ACT.Copy, scale=ZS).then_inc(heads_whole_in.sem, 1)
                elif what == "shift":
                    act.wait_ge(shift_turned.sem, shift_turned.at(b, k))
                    act.wait_ge(heads_lo_in.sem, heads_lo_in.at(b, 2 * k + 1))
                    past, which_k = shift_moved.before(b, k, 1)
                    if begun(past):
                        act.wait_ge(shift_moved.sem, shift_moved.at(past, which_k))
                    a.activation(shift_rows[:], G[:].bitcast(F16)[0:2 * NB, 0:P], ACT.Copy).then_inc(shift_in.sem, 1)
                elif what == "zl":
                    act.wait_ge(late_projected.sem, late_projected.at(b))
                    if begun(b - 1):
                        act.wait_ge(logits_ready.sem, logits_ready.at(b - 1, NB - 1))
                    a.activation(zl_t[:, 0, :], G[:], ACT.Copy, scale=ZS).then_inc(late_hi_in.sem, 1)
                elif what == "vl":
                    act.wait_ge(values_ready.sem, values_ready.at(b))
                    if begun(b - 1):
                        act.wait_ge(late_contexts.sem, late_contexts.at(b - 1))
                    a.activation(v_l[:].rearrange("p n d -> p (n d)"), G[:, 0:NB * D], ACT.Copy).then_inc(values_in.sem, 1)
                elif what == "hid" and k == HB - 1:
                    if begun(b - 1):
                        act.wait_ge(experts0_ready.sem, experts0_ready.at(b - 1, NB - 1))
                    for m in range(HB):
                        act.wait_ge(hidden_ready.sem, hidden_ready.at(b, m))
                        a.activation(hid[:, m, :], g_bank[(at - (HB - 1 - m)) % G_BANKS][:], ACT.Gelu,
                                     bias=b1_c[:, m:m + 1], scale=hid_scale[:, 0:1]).then_inc(hidden_in.sem, 1)
                elif what == "rh":
                    act.wait_ge(router_hidden.sem, router_hidden.at(b))
                    if begun(b - 1):
                        act.wait_ge(router_logits.sem, router_logits.at(b - 1))
                    a.activation(r_hid[:], G[0:RH, :], ACT.Relu, bias=rb1_c[:, 0:1]).then_inc(router_hidden_in.sem, 1)
                elif what == "e1":
                    act.wait_ge(layer1_ready.sem, layer1_ready.at(b, k))
                    if begun(b - 1):
                        act.wait_ge(layer2_ready.sem, layer2_ready.at(b - 1, k))
                    a.activation(e1_t[:, k, :], G[:], ACT.Relu, bias=eb1_c[:, k:k + 1]).then_inc(layer1_in.sem, 1)
                elif what == "e2":
                    act.wait_ge(layer2_ready.sem, layer2_ready.at(b, k))
                    if begun(b - 1):
                        act.wait_ge(experts1_ready.sem, experts1_ready.at(b - 1, NB - 1))
                    a.activation(e2_t[:, k, :], G[:], ACT.Relu, bias=eb2_c[:, k:k + 1]).then_inc(layer2_in.sem, 1)

            def exp(b, m):
                act.wait_ge(scores_ready.sem, scores_ready.at(b, m))
                past, which_k = contexts_ready.before(b, m // 2, NB)
                if begun(past):
                    act.wait_ge(contexts_ready.sem, contexts_ready.at(past, which_k))
                h = 2 * (m // (2 * NB)) + m % 2
                a.activation(probs[m % 8][:], s_bank[m % 2][:], ACT.Exp,
                             scale=exp_scale[:, h:h + 1]).then_inc(probs_ready.sem, 1)

            def store_context(b, p):
                act.wait_ge(contexts_ready.sem, contexts_ready.at(b, NB * p + NB - 1))
                if begun(b - 1):
                    act.wait_ge(attended.sem, attended.at(b - 1, NB - 1))
                if begun(b - 1):
                    act.wait_ge(sums_moved.sem, sums_moved.at(b - 1, p))
                a.activation(context[:, p, :], c_bank[p % C_BANKS][:], ACT.Copy).then_inc(contexts_in.sem, 1)

            def body(i, parity):
                for n in range(SLOTS):
                    mine = turns_of(n)
                    for turn in mine[:BEFORE_EXP[n]]:
                        if active(i, turn[1]):
                            store_turn(i, parity, *turn)
                    if n >= 1 and active(i, "attn"):
                        exp(i - 1, n - 1)
                    if n == 0 and active(i, "mid"):
                        exp(i - 2, SLOTS - 1)
                    if n % 8 == STEP_AT["store_context"] and n >= 8 and active(i, "attn"):
                        store_context(i - 1, n // 8 - 1)
                    if n == STEP_AT["store_context"] and active(i, "mid"):
                        store_context(i - 2, PAIRS - 1)
                    for turn in mine[BEFORE_EXP[n]:]:
                        if active(i, turn[1]):
                            store_turn(i, parity, *turn)
                    if n == STEP_AT["gate_exp"] and active(i, "mid"):
                        act.wait_ge(gate_offsets.sem, gate_offsets.at(i - 2))
                        a.activation(g_exp[:], g_off[:], ACT.Exp).then_inc(gate_exp.sem, 1)
                    if n == STEP_AT["router_exp"] and active(i, "late"):
                        act.wait_ge(router_offsets.sem, router_offsets.at(i - 3))
                        a.activation(r_exp[:], r_off[:], ACT.Exp).then_inc(router_exp.sem, 1)
                    if n == STEP_AT["second_exp"] and active(i, "late"):
                        act.wait_ge(gap_ready.sem, gap_ready.at(i - 3))
                        a.activation(r_e2[:], r_gap[:], ACT.Exp).then_inc(router_exp.sem, 1)

            each_iteration(act, body, after_second=lambda: act.wait_ge(ready, 1))

        @block.vector
        def _(dve):
            v = nc.vector
            n_setup = 0

            def setup(ins):
                nonlocal n_setup
                ins.then_inc(dve_setup, 1)
                n_setup += 1
                dve.wait_ge(dve_setup, n_setup)

            def over(ap, shape):
                return ap.broadcast_to(shape)

            def largest(columns):
                nonlocal n_peaks
                n_peaks += 1
                n = columns.stop - columns.start
                dve.wait_ge(amax_turned, n_peaks)
                setup(v.reduce_max(top[0:n], c_bank[0][0:n, 0:P], axis=AX))
                v.tensor_tensor(peak[0:n, 0:n], id32[0:n, 0:n], over(top[0:n], [n, n]), ALU.mult).then_inc(peak_ready, 1)
                dve.wait_ge(sigma_ready, n_peaks)
                setup(v.tensor_scalar(sigma[:, columns], c_bank[0][:, P:P + n], TINY, None, ALU.max))
                setup(v.reciprocal(rsigma[:, columns], sigma[:, columns]))
                setup(v.tensor_scalar(rsigma[:, columns], rsigma[:, columns], WS, None, ALU.mult))

            n_peaks = 0
            dve.wait_ge(front_weights_in, 16 * FRONT_LOADS)
            dve.wait_ge(consts_made, 1)
            setup(v.tensor_copy(q_first[:], q_dup[:, :, :, 0:1]))
            setup(v.tensor_copy(k_first[:], k_raw[:, :, 0:1]))
            setup(v.tensor_tensor(q_dup[:], q_dup[:], over(q_first[:], [R0, H0, 2, D]), ALU.subtract))
            v.tensor_tensor(k_raw[:], k_raw[:], over(k_first[:], [R0, H0, D]), ALU.subtract).then_inc(first_off, 1)
            v.tensor_scalar(bn_raw[:, 2, :], bn_raw[:, 2, :], BN_EPS, None, ALU.add).then_inc(bn_var, 1)
            setup(v.tensor_tensor(bn_raw[:, 0, :], bn_raw[:, 0, :], bn_raw[:, 1, :], ALU.subtract))
            setup(v.tensor_scalar(k_sign[:], k_raw0[:], 0.0, 0.5, ALU.is_ge, ALU.subtract))
            heads = s_bank[0][:].rearrange("p (h d) -> p h d", h=H0)
            dve.wait_ge(heads_folded, 1)
            v.tensor_reduce(amax[:, 0:H0], heads, axis=AX, op=ALU.max,
                            apply_absolute_value=True).then_inc(amax_ready, 1)
            largest(slice(0, H0))
            setup(v.tensor_scalar(exp_scale[:], sigma[:, 0:H0], 1.0 / (LOGIT * D ** 0.5), None, ALU.mult))
            setup(v.tensor_tensor(a_nrm[:], heads, over(rsigma[:, 0:H0, None], [P, H0, D]), ALU.mult))
            for c in range(2):
                setup(v.tensor_copy(a_w[:, :, 0, c, :], a_nrm[:]))
                last = v.tensor_tensor(a_w[:, :, 1, c, :], a_nrm[:], a_w[:, :, 0, c, :], ALU.subtract)
            last.then_inc(front_ready, 1)
            dve.wait_ge(bn_pow, 1)
            setup(v.tensor_scalar(bn_scale[:], bn_inv[:], 4.0, None, ALU.mult))
            setup(v.tensor_tensor(bn_shift[:], bn_raw[:, 0, :], bn_inv[:], ALU.mult))
            setup(v.tensor_tensor(bn_shift[:], bn_shift[:], bn_raw[:, 3, :], ALU.add))

            def setup_rest():
                dve.wait_ge(weights_in, 16 * (MORE_LOADS + ACT_LOADS))
                dve.wait_ge(consts_made, 2)
                setup(v.tensor_copy(row_part[:, 0, :], row[:]))
                setup(v.tensor_tensor(row_rest[:, 0, :], row[:], row_part[:, 0, :], ALU.subtract))
                setup(v.tensor_copy(row_part[:, 1, :], row_rest[:, 0, :]))
                setup(v.tensor_tensor(row_rest[:, 1, :], row_rest[:, 0, :], row_part[:, 1, :], ALU.subtract))
                v.tensor_copy(row_part[:, 2, :], row_rest[:, 1, :]).then_inc(rows_split, 1)
                dve.wait_ge(folded, 1)
                v.tensor_copy(wo_t[:], c_bank[0][0:D, 0:D]).then_inc(wo_ready, 1)
                dve.wait_ge(folded, 2)
                setup(v.tensor_copy(w_raw[:, W_Z:W_R], c_bank[0][:, 2 * P:3 * P]))
                for s, (lo, hi) in enumerate(SEGMENTS):
                    last = v.tensor_reduce(amax[:, H0 + s:H0 + s + 1], w_raw[:, lo:hi], axis=AX, op=ALU.max,
                                           apply_absolute_value=True)
                last.then_inc(amax_ready, 1)
                for c in range(2):
                    half = slice(D * c, D * c + D)
                    setup(v.tensor_tensor(vo_w[half, :, half], vo_w[half, :, half], vo_first[half, :, :], ALU.subtract))
                setup(v.tensor_scalar(vo_w[:], vo_w[:], 1.0 / XS, None, ALU.mult))
                largest(slice(H0, N_SG))
                for s, (lo, hi) in enumerate(SEGMENTS):
                    setup(v.tensor_scalar(w_nrm[:, lo:hi], w_raw[:, lo:hi], rsigma[:, H0 + s:H0 + s + 1], None, ALU.mult))
                setup(v.tensor_copy(w_hi[:], w_nrm[:]))
                setup(v.tensor_tensor(w_lo[:], w_nrm[:], w_hi[:], ALU.subtract))
                for c in range(2):
                    v.tensor_copy(z_w[:, 0, c, :], w_hi[:, W_Z:W_V])
                    v.tensor_copy(z_w[:, 1, c, :], w_lo[:, W_Z:W_V])
                setup(v.tensor_scalar(unscale[:], sigma[:], 1.0 / LIN, None, ALU.mult))
                setup(v.tensor_scalar(rescale[:], rsigma[:], LIN / WS, None, ALU.mult))
                v.tensor_copy(hid_scale[:], unscale[:, SG_HID:SG_HID + 1])
                v.tensor_scalar(rb1_c[:], rb1_c[:], rescale[0:RH, SG_R:SG_R + 1], None, ALU.mult)
                v.tensor_scalar(rw2_w[:], rw2_w[:], unscale[0:RH, SG_R:SG_R + 1], None, ALU.mult)
                v.tensor_scalar(eb1_c[:], eb1_c[:], rescale[:, SG_E:SG_E + 1], None, ALU.mult)
                v.tensor_scalar(e2_w[:], e2_w[:], unscale[:, SG_E:SG_E + 1], None, ALU.mult)
                setup(v.tensor_copy(row_scale[:], row_no[:]))
                setup(v.tensor_scalar(row_scale[:], row_scale[:], 1.0, None, ALU.max))
                setup(v.reciprocal(row_scale[:], row_scale[:]))
                setup(v.tensor_scalar(row_scale[:], row_scale[:], sigma[:, SG_Z:SG_Z + 1], 1.0 / LOGIT, ALU.mult, ALU.mult))
                setup(v.tensor_scalar(row_scale[:], row_scale[:], unscale[:, SG_V:SG_V + 1], None, ALU.mult))
                v.tensor_copy(rank[:], rank_i[:]).then_inc(ready, 1)

            def ln_centre(chain, b, which, src):
                w = ln[which - 1]
                chain.link(dve, b, v.reduce_sum(w["sum"][:], src[:], axis=AX))
                chain.link(dve, b, v.tensor_scalar(w["mu"][:], w["sum"][:], -1.0 / D, None, ALU.mult))
                chain.link(dve, b, v.tensor_tensor(w["d"][:], src[:], over(w["mu"][:, :, None], [P, NB, D]), ALU.add))

            def ln_var(chain, b, which):
                w = ln[which - 1]
                chain.link(dve, b, v.tensor_tensor(w["sq"][:], w["d"][:], w["d"][:], ALU.mult))
                chain.link(dve, b, v.reduce_sum(w["sum2"][:], w["sq"][:], axis=AX))
                v.tensor_scalar(w["var"][:], w["sum2"][:], 1.0 / (D * XS * XS), LN_EPS / (XS * XS),
                                ALU.mult, ALU.add).then_inc(var_ready[which].sem, 1)

            def ln_parts(chain, b, which, dst):
                w = ln[which - 1]
                dve.wait_ge(factor_ready[which].sem, factor_ready[which].at(b))
                if begun(b - 1):
                    dve.wait_ge(rows_turned[which].sem, rows_turned[which].at(b - 1))
                f = slice(1 if which == 1 else 0, D)
                f_lo = slice(D + f.start, 2 * D)
                chain.link(dve, b, v.tensor_tensor(dst[:, :, f], w["d"][:, :, f],
                                                   over(w["r"][:, :, None], [P, NB, D - f.start]), ALU.mult))
                chain.link(dve, b, v.tensor_copy(w["parts"][:, :, f], dst[:, :, f]))
                v.tensor_tensor(w["parts"][:, :, f_lo], dst[:, :, f], w["parts"][:, :, f],
                                ALU.subtract).then_inc(parts_ready[which].sem, 1)

            def ranked(n):
                return over(rank[:, None, 0:n], [P, NB, n])

            def store_turn(i, parity, at, stage, what, k):
                b = i - LAG[stage]
                G = g_bank[at % G_BANKS]
                if what == "zl":
                    dve.wait_ge(late_hi_in.sem, late_hi_in.at(b))
                    v.scalar_tensor_tensor(out=zl_t[:, 1, :], in0=G[:], scalar=ZS, in1=zl_t[:, 0, :],
                                           op0=ALU.mult, op1=ALU.subtract).then_inc(late_lo_in.sem, 1)
                elif what == "conv":
                    dve.wait_ge(conv_done.sem, conv_done.at(b))
                    if begun(b - 2):
                        dve.wait_ge(h1_ready.sem, h1_ready.at(b - 2, NB - 1))
                    h = h0[parity]
                    v.tensor_tensor(h[:], G[:, 0:NB * D].rearrange("p (n d) -> p n d", n=NB),
                                    over(bn_scale[:, None, :], [P, NB, D]), ALU.mult).then_inc(conv_in.sem, 1)
                    dve.wait_ge(conv_in.sem, conv_in.at(b))
                    ve_front.link(dve, b, v.tensor_tensor(h[:], h[:], over(bn_shift[:, None, :], [P, NB, D]), ALU.add))
                elif what == "vo":
                    dve.wait_ge(attended.sem, attended.at(b, k))
                    past, which_k = h1_ready.before(b, k, 2)
                    if begun(past):
                        dve.wait_ge(h1_ready.sem, h1_ready.at(past, which_k))
                    inv = row_inv[:, k * H0:(k + 1) * H0, None]
                    v.tensor_tensor(vo_tmp[k % 2][:], G[:].rearrange("p (h d) -> p h d", h=H0),
                                    over(inv, [P, H0, D]), ALU.mult).then_inc(attended_in.sem, 1)
                elif what == "sums":
                    dve.wait_ge(sums_ready.sem, sums_ready.at(b))
                    v.reciprocal(row_inv[:], G[:, 0:SLOTS]).then_inc(sums_inverted.sem, 1)
                    dve.wait_ge(sums_inverted.sem, sums_inverted.at(b))
                elif what == "gate":
                    dve.wait_ge(gate_logits.sem, gate_logits.at(b))
                    logits = G[:, 0:NB * E0].rearrange("p (n e) -> p n e", n=NB)
                    ve_mid.link(dve, b, v.reduce_max(g_max[:], logits, axis=AX))
                    v.tensor_tensor(g_off[:], logits, over(g_max[:, :, None], [P, NB, E0]),
                                    ALU.subtract).then_inc(gate_offsets.sem, 1)
                elif what == "y":
                    dve.wait_ge(experts0_ready.sem, experts0_ready.at(b, k))
                    past, which_k = h2_ready.before(b, k, 2)
                    if begun(past):
                        dve.wait_ge(h2_ready.sem, h2_ready.at(past, which_k))
                    if k == 0:
                        dve.wait_ge(gate_ready.sem, gate_ready.at(b))
                    v.tensor_tensor(y_tmp[k % 2][:], G[:].rearrange("p (e d) -> p e d", e=E0),
                                    over(gate[:, k, :, None], [P, E0, D]), ALU.mult).then_inc(experts0_in.sem, 1)
                elif what == "lg":
                    dve.wait_ge(logits_ready.sem, logits_ready.at(b, k))
                    if k == 0:
                        if begun(b - 1):
                            dve.wait_ge(late_contexts.sem, late_contexts.at(b - 1))
                    wide = 512 - k * P
                    v.scalar_tensor_tensor(out=att_t[:, k, k * P:512], in0=G[:, 0:wide], scalar=0.0,
                                           in1=causal[:, 0:wide], op0=ALU.max, op1=ALU.mult).then_inc(logits_in.sem, 1)
                elif what == "av":
                    dve.wait_ge(late_contexts.sem, late_contexts.at(b))
                    v.tensor_tensor(av_tmp[:], G[:, 0:NB * D].rearrange("p (n d) -> p n d", n=NB),
                                    over(row_scale[:, :, None], [P, NB, D]), ALU.mult).then_inc(late_contexts_in.sem, 1)
                    dve.wait_ge(late_contexts_in.sem, late_contexts_in.at(b))
                    if begun(b - 1):
                        dve.wait_ge(out_ready.sem, out_ready.at(b - 1, NB - 1))
                    dve.wait_ge(h2_ready.sem, h2_ready.at(b, NB - 1))
                    v.tensor_tensor(h3[:], av_tmp[:], h2[:], ALU.add).then_inc(h3_ready.sem, 1)
                    dve.wait_ge(h3_ready.sem, h3_ready.at(b))
                elif what == "rl":
                    dve.wait_ge(router_logits.sem, router_logits.at(b))
                    logits = G[:, 0:NB * E1].rearrange("p (n e) -> p n e", n=NB)
                    ve_late.link(dve, b, v.reduce_max(r_max[:], logits, axis=AX))
                    v.tensor_tensor(r_off[:], logits, over(r_max[:, :, None], [P, NB, E1]),
                                    ALU.subtract).then_inc(router_offsets.sem, 1)
                elif what == "o":
                    dve.wait_ge(experts1_ready.sem, experts1_ready.at(b, k))
                    past, which_k = out_ready.before(b, k, 2)
                    if begun(past):
                        dve.wait_ge(out_ready.sem, out_ready.at(past, which_k))
                    if k == 0:
                        dve.wait_ge(route_ready.sem, route_ready.at(b))
                    v.tensor_tensor(o_tmp[k % 2][:], G[:, 0:E1 * D].rearrange("p (e d) -> p e d", e=E1),
                                    over(r_gate[:, k, :, None], [P, E1, D]), ALU.mult).then_inc(experts1_in.sem, 1)

            def finish_gate(b):
                def link(ins):
                    ve_mid.link(dve, b, ins)
                dve.wait_ge(gate_exp.sem, gate_exp.at(b))
                link(v.reduce_sum(g_sum[:], g_exp[:], axis=AX))
                link(v.reciprocal(g_inv[:], g_sum[:]))
                link(v.scalar_tensor_tensor(out=g_key[:], in0=g_off[:], scalar=0.0, in1=ranked(E0), op0=ALU.is_ge, op1=ALU.mult))
                link(v.reduce_max(g_top[:], g_key[:], axis=AX))
                link(v.tensor_tensor(g_hot[:], g_key[:], over(g_top[:, :, None], [P, NB, E0]), ALU.is_equal))
                v.tensor_tensor(gate[:], g_hot[:], over(g_inv[:, :, None], [P, NB, E0]), ALU.mult).then_inc(gate_ready.sem, 1)

            def route(b):
                def link(ins):
                    ve_late.link(dve, b, ins)
                dve.wait_ge(router_exp.sem, router_exp.at(b, 0))
                link(v.reduce_sum(r_sum[:], r_exp[:], axis=AX))
                link(v.reciprocal(r_inv[:], r_sum[:]))
                link(v.tensor_tensor(r_p[:], r_exp[:], over(r_inv[:, :, None], [P, NB, E1]), ALU.mult))
                link(v.scalar_tensor_tensor(out=r_key[:], in0=r_off[:], scalar=0.0, in1=ranked(E1), op0=ALU.is_ge, op1=ALU.mult))
                link(v.reduce_max(r_top[:], r_key[:], axis=AX))
                link(v.tensor_tensor(r_hot[:], r_key[:], over(r_top[:, :, None], [P, NB, E1]), ALU.is_equal))
                link(v.scalar_tensor_tensor(out=r_rest[:], in0=r_hot[:], scalar=-2.0, in1=r_p[:], op0=ALU.mult, op1=ALU.add))

            def route_second(b):
                def link(ins):
                    ve_late.link(dve, b, ins)
                link(v.reduce_max(r_second[:], r_rest[:], axis=AX))
                link(v.tensor_tensor(r_is2[:], r_rest[:], over(r_second[:, :, None], [P, NB, E1]), ALU.is_equal))
                link(v.tensor_tensor(r_key2[:], r_is2[:], ranked(E1), ALU.mult))
                link(v.reduce_max(r_top2[:], r_key2[:], axis=AX))
                link(v.tensor_tensor(r_hot2[:], r_key2[:], over(r_top2[:, :, None], [P, NB, E1]), ALU.is_equal))
                v.tensor_tensor(r_gap[:], r_second[:], r_inv[:], ALU.subtract).then_inc(gap_ready.sem, 1)

            def finish_route(b):
                def link(ins):
                    ve_late.link(dve, b, ins)
                dve.wait_ge(router_exp.sem, router_exp.at(b, 1))
                link(v.tensor_scalar(r_den[:], r_e2[:], 1.0, None, ALU.add))
                link(v.reciprocal(r_w1[:], r_den[:]))
                link(v.tensor_tensor(r_w2[:], r_w1[:], r_e2[:], ALU.mult))
                link(v.tensor_tensor(r_g1[:], r_hot[:], over(r_w1[:, :, None], [P, NB, E1]), ALU.mult))
                link(v.tensor_tensor(r_g2[:], r_hot2[:], over(r_w2[:, :, None], [P, NB, E1]), ALU.mult))
                v.tensor_tensor(r_gate[:], r_g1[:], r_g2[:], ALU.add).then_inc(route_ready.sem, 1)

            def body(i, parity):
                for n in range(SLOTS):
                    mine = turns_of(n)
                    for turn in mine[:BEFORE_MAX[n]]:
                        if active(i, turn[1]):
                            store_turn(i, parity, *turn)
                    m, b = (n + M_AHEAD) % SLOTS, i if n + M_AHEAD >= SLOTS else i - LAG["attn"]
                    if active(i, "front" if b is i else "attn"):
                        dve.wait_ge(scores_for_max.sem, scores_for_max.at(b, m))
                        if m % (2 * NB) == 0 and begun(b - 1):
                            dve.wait_ge(shift_ready.sem, shift_ready.at(b - 1, m // (2 * NB)))
                        v.tensor_reduce(neg_max[:, m:m + 1], m_bank[m % M_BANKS][:, 0:T], axis=AX, op=ALU.max,
                                        negate=True).then_inc(max_ready.sem, 1)
                    for turn in mine[BEFORE_MAX[n]:]:
                        if active(i, turn[1]):
                            store_turn(i, parity, *turn)
                    if active(i, "front"):
                        if n == STEP_AT["signs"]:
                            dve.wait_ge(x_loaded.sem, x_loaded.at(i))
                            if begun(i - 1):
                                dve.wait_ge(x_turned.sem, x_turned.at(i - 1))
                            v.tensor_scalar(x_sign[:], x_in[:], 0.0, 0.5, ALU.is_ge, ALU.subtract).then_inc(signs_ready.sem, 1)
                        if n == STEP_AT["centre1"]:
                            ln_centre(ve_front, i, 1, h0[parity])
                        if n == STEP_AT["var1"]:
                            ln_var(ve_front, i, 1)
                        if n == STEP_AT["parts1"]:
                            if begun(i - 2):
                                dve.wait_ge(contexts_ready.sem, contexts_ready.at(i - 2, SLOTS // 2 - 1))
                            ln_parts(ve_front, i, 1, xn1[parity])
                    if active(i, "mid"):
                        b = i - LAG["mid"]
                        if n == STEP_AT["centre2"]:
                            dve.wait_ge(h1_ready.sem, h1_ready.at(b, NB - 1))
                            ln_centre(ve_mid, b, 2, h1)
                        if n == STEP_AT["var2"]:
                            ln_var(ve_mid, b, 2)
                        if n == STEP_AT["parts2"]:
                            ln_parts(ve_mid, b, 2, xn_other[0])
                        if n == STEP_AT["gate"]:
                            finish_gate(b)
                        if n == STEP_AT["centre3"]:
                            dve.wait_ge(h2_ready.sem, h2_ready.at(b, NB - 1))
                            ln_centre(ve_mid, b, 3, h2)
                        if n == STEP_AT["var3"]:
                            ln_var(ve_mid, b, 3)
                        if n == STEP_AT["parts3"]:
                            ln_parts(ve_mid, b, 3, xn_other[1])
                    if active(i, "late"):
                        b = i - LAG["late"]
                        if n == STEP_AT["centre4"]:
                            ln_centre(ve_late, b, 4, h3)
                        if n == STEP_AT["var4"]:
                            ln_var(ve_late, b, 4)
                        if n == STEP_AT["parts4"]:
                            ln_parts(ve_late, b, 4, xn_other[2])
                        if n == STEP_AT["route"]:
                            route(b)
                        if n == STEP_AT["second"]:
                            route_second(b)
                        if n == STEP_AT["route_end"]:
                            finish_route(b)
                if active(i, "front"):
                    ve_front.end()
                if active(i, "mid"):
                    ve_mid.end()
                if active(i, "late"):
                    ve_late.end()

            each_iteration(dve, body, after_first=setup_rest, after_second=lambda: dve.wait_ge(ready, 1))

        @block.tensor
        def _(pe):
            t_ = nc.tensor

            def product(dst, pairs, start=True):
                for n, (lhs, rhs) in enumerate(pairs):
                    last = t_.matmul(dst, lhs, rhs, start=start and n == 0, stop=n == len(pairs) - 1,
                                     skip_group_check=True)
                return last

            def largest(columns):
                nonlocal n_peaks
                n_peaks += 1
                n = columns.stop - columns.start
                pe.wait_ge(amax_ready, n_peaks)
                t_.transpose(c_bank[0][0:n, 0:P], amax[:, columns], id32[:]).then_inc(amax_turned, 1)
                pe.wait_ge(peak_ready, n_peaks)
                product(c_bank[0][:, P:P + n], [(ones32[0:n, :], peak[0:n, 0:n])]).then_inc(sigma_ready, 1)

            n_peaks = 0
            pe.wait_ge(front_weights_in, 16 * FRONT_LOADS)
            pe.wait_ge(consts_made, 1)
            pe.wait_ge(first_off, 1)
            for h in range(H0):
                last = product(s_bank[0][:, h * D:(h + 1) * D],
                               [(q_dup[:, h, :, :].rearrange("r c d -> r (c d)"), k_raw[:, h, :])])
            last.then_inc(heads_folded, 1)
            largest(slice(0, H0))
            pe.wait_ge(front_ready, 1)

            def setup_rest():
                pe.wait_ge(weights_in, 16 * (MORE_LOADS + ACT_LOADS))
                t_.transpose(c_bank[0][0:D, 0:D], wo_raw[:], id32[0:D, 0:D]).then_inc(folded, 1)
                pe.wait_ge(wo_ready, 1)
                product(c_bank[0][:, 2 * P:2 * P + D], [(wq_dup[:].rearrange("c s d -> c (s d)"), wk_raw[:])])
                product(c_bank[0][:, 2 * P + D:3 * P],
                        [(wv_dup[:].rearrange("c s d -> c (s d)"), wo_t[:])]).then_inc(folded, 1)
                largest(slice(H0, N_SG))

            def weights_ready():
                pe.wait_ge(ready, 1)
                pe.wait_ge(rows_in, 48)

            def stacked(lo, hi, xt, lhs=True):
                return [(w[:, lo:hi], xt) if lhs else (xt, w[:, lo:hi]) for w in (w_hi, w_lo)]

            def turn(i, parity, at, stage, what, k):
                b = i - LAG[stage]
                G, read_out = g_bank[at % G_BANKS], last_use(i, at)
                blk = slice(k * P, (k + 1) * P)
                if what == "xq":
                    pe.wait_ge(signs_ready.sem, signs_ready.at(b))
                    pe.wait_ge(*read_out)
                    for n in range(NB):
                        last = t_.transpose(G[:].bitcast(BF16)[:, n * P:(n + 1) * P], x_sign[:, n, :], idb[:])
                    last.then_inc(x_turned.sem, 1)
                elif what == "conv":
                    pe.wait_ge(x_turned_in.sem, x_turned_in.at(b))
                    pe.wait_ge(*read_out)
                    for n in range(NB):
                        last = product(G[:, n * D:(n + 1) * D],
                                       [(xq_t[:, n * P + s:n * P + s + P], k_sign[:, s, :]) for s in range(TAPS)])
                    last.then_inc(conv_done.sem, 1)
                elif what in ("xt1", "xt2", "xt3", "xt4"):
                    which = int(what[2])
                    w = ln[which - 1]["parts"]
                    pe.wait_ge(parts_ready[which].sem, parts_ready[which].at(b))
                    pe.wait_ge(*read_out)
                    for n in range(NB):
                        last = t_.transpose(G[:].bitcast(F16)[:, n * P:(n + 1) * P], w[:, n, :], id16[:])
                    last.then_inc(rows_turned[which].sem, 1)
                elif what == "z":
                    if k == 0:
                        pe.wait_ge(rows1_in.sem, rows1_in.at(b))
                    pe.wait_ge(*read_out)
                    par = parity if stage == "front" else 1 - parity
                    last = product(G[:], [(a_w[:, k, s].rearrange("p c d -> p (c d)"), xt1[par][:]) for s in range(2)])
                    last.then_inc(heads_projected.sem, 1)
                elif what == "shift":
                    pe.wait_ge(shift_ready.sem, shift_ready.at(b, k))
                    pe.wait_ge(*read_out)
                    t_.transpose(G[:].bitcast(F16)[0:2 * NB, 0:P], shift[:, 2 * NB * k:2 * NB * (k + 1)],
                                 id16[:]).then_inc(shift_turned.sem, 1)
                elif what == "sums":
                    pe.wait_ge(sums_moved.sem, sums_moved.at(b, PAIRS - 1))
                    pe.wait_ge(*read_out)
                    for n in range(NB):
                        last = product(G[:, n * H0:(n + 1) * H0],
                                       [(sum_rows[:, n * P:(n + 1) * P], id32[0:H0, 0:H0])])
                    last.then_inc(sums_ready.sem, 1)
                elif what == "vo":
                    if k == 0:
                        pe.wait_ge(contexts_in.sem, contexts_in.at(b, PAIRS - 1))
                    pe.wait_ge(*read_out)
                    for p in range(PAIRS):
                        last = product(G[:, p * P:(p + 1) * P], [(context[:, p, blk], vo_w[:, p, :])])
                    last.then_inc(attended.sem, 1)
                elif what == "hid":
                    if k == 0:
                        pe.wait_ge(rows2_in.sem, rows2_in.at(b))
                    pe.wait_ge(*read_out)
                    last = product(G[:], stacked(k * P, (k + 1) * P, xt2[:]))
                    last.then_inc(hidden_ready.sem, 1)
                elif what == "gate":
                    pe.wait_ge(hidden_in.sem, hidden_in.at(b, HB - 1))
                    pe.wait_ge(*read_out)
                    t_.matmul(G[:, 0:NB * E0], ones_rows[:], bias_rows[:, R_G:R_L], start=True, stop=False,
                              skip_group_check=True)
                    for n in range(NB):
                        last = product(G[:, n * E0:(n + 1) * E0],
                                       [(hid[:, m, n * P:(n + 1) * P], wg_w[:, m, :]) for m in range(HB)], start=False)
                    last.then_inc(gate_logits.sem, 1)
                elif what == "y":
                    pe.wait_ge(*read_out)
                    last = product(G[:], [(ones_rows[:], bias_rows[:, R_D:R_3])]
                                   + [(hid[:, m, blk], wd_w[:, m, :]) for m in range(HB)])
                    last.then_inc(experts0_ready.sem, 1)
                elif what == "zl":
                    pe.wait_ge(rows3_in.sem, rows3_in.at(b))
                    pe.wait_ge(*read_out)
                    last = product(G[:], [(z_w[:, s].rearrange("p c d -> p (c d)"), xt3[:]) for s in range(2)])
                    last.then_inc(late_projected.sem, 1)
                elif what == "vl":
                    pe.wait_ge(*read_out)
                    for n in range(NB):
                        last = product(G[:, n * D:(n + 1) * D], stacked(W_V, W_R, xt3[:, n * P:(n + 1) * P], lhs=False))
                    last.then_inc(values_ready.sem, 1)
                elif what == "lg":
                    if k == 0:
                        pe.wait_ge(late_lo_in.sem, late_lo_in.at(b))
                    pe.wait_ge(*read_out)
                    last = product(G[:, 0:512 - k * P], [(xt3[:, blk], zl_t[:, s, k * P:512]) for s in range(2)])
                    last.then_inc(logits_ready.sem, 1)
                elif what == "av":
                    pe.wait_ge(logits_in.sem, logits_in.at(b, NB - 1))
                    pe.wait_ge(values_in.sem, values_in.at(b))
                    pe.wait_ge(*read_out)
                    for n in range(NB):
                        last = product(G[:, n * D:(n + 1) * D],
                                       [(att_t[:, j, n * P:(n + 1) * P], v_l[:, j, :]) for j in range(n + 1)])
                    last.then_inc(late_contexts.sem, 1)
                elif what == "rh":
                    pe.wait_ge(rows4_in.sem, rows4_in.at(b))
                    pe.wait_ge(*read_out)
                    last = product(G[0:RH, :], stacked(W_R, W_E, xt4[:]))
                    last.then_inc(router_hidden.sem, 1)
                elif what == "rl":
                    pe.wait_ge(router_hidden_in.sem, router_hidden_in.at(b))
                    pe.wait_ge(*read_out)
                    t_.matmul(G[:, 0:NB * E1], ones_rows[:], bias_rows[:, R_L:R_ALL], start=True, stop=False,
                              skip_group_check=True)
                    for n in range(NB):
                        last = product(G[:, n * E1:(n + 1) * E1], [(r_hid[:, n * P:(n + 1) * P], rw2_w[:])], start=False)
                    last.then_inc(router_logits.sem, 1)
                elif what == "e1":
                    pe.wait_ge(*read_out)
                    last = product(G[:], stacked(W_E + k * P, W_E + (k + 1) * P, xt4[:]))
                    last.then_inc(layer1_ready.sem, 1)
                elif what == "e2":
                    pe.wait_ge(layer1_in.sem, layer1_in.at(b, k))
                    pe.wait_ge(*read_out)
                    last = product(G[:], [(e2_w[:, k, :], e1_t[:, k, :])])
                    last.then_inc(layer2_ready.sem, 1)
                elif what == "o":
                    if k == 0:
                        pe.wait_ge(layer2_in.sem, layer2_in.at(b, EP - 1))
                    pe.wait_ge(*read_out)
                    t_.matmul(G[:, 0:E1 * D], ones_rows[:], bias_rows[:, R_3:R_G], start=True, stop=False,
                              skip_group_check=True)
                    for p in range(EP):
                        last = product(G[:, p * P:(p + 1) * P], [(e2_t[:, p, blk], e3_w[:, p, :])], start=False)
                    last.then_inc(experts1_ready.sem, 1)

            def scores_max(b, par, m):
                h, t = divmod(m, NB)
                if t == 0:
                    pe.wait_ge(heads_hi_in.sem, heads_hi_in.at(b, h))
                past, which_k = max_ready.before(b, m, M_BANKS)
                if begun(past):
                    pe.wait_ge(max_ready.sem, max_ready.at(past, which_k))
                product(m_bank[m % M_BANKS][:, 0:T], [(z_t[h][:, 0, t * P:(t + 1) * P], xt1[par][:, 0:T])])\
                    .then_inc(scores_for_max.sem, 1)

            def scores(b, par, n):
                p, j, s = n // (2 * NB), n // 2 % NB, n % 2
                h = 2 * p + s
                if j == 0 and s == 0:
                    pe.wait_ge(shift_moved.sem, shift_moved.at(b, p))
                past, which_k = probs_ready.before(b, n, 2)
                if begun(past):
                    pe.wait_ge(probs_ready.sem, probs_ready.at(past, which_k))
                product(s_bank[n % 2][:], [(xt1[par][:, j * P:(j + 1) * P], z_t[h][:, c, :]) for c in range(2)])\
                    .then_inc(scores_ready.sem, 1)

            def contexts(b, par, p, j):
                first = 2 * NB * p + 2 * j
                pe.wait_ge(probs_ready.sem, probs_ready.at(b, first + 1))
                if j == 0:
                    past, which_k = contexts_in.before(b, p, C_BANKS)
                    if begun(past):
                        pe.wait_ge(contexts_in.sem, contexts_in.at(past, which_k))
                keys = P if j < NB - 1 else TAIL
                for s in range(2):
                    last = t_.matmul(c_bank[p % C_BANKS][s * D:(s + 1) * D, :], xn1[par][0:keys, j, :], probs[(first + s) % 8][0:keys, :],
                                     start=j == 0, stop=j == NB - 1, skip_group_check=True)
                last.then_inc(contexts_ready.sem, 1)

            def body(i, parity):
                for n in range(SLOTS):
                    mine = turns_of(n)
                    for turn_ in mine[:BEFORE_SCORES[n]]:
                        if active(i, turn_[1]):
                            turn(i, parity, *turn_)
                    if active(i, "attn"):
                        scores(i - 1, 1 - parity, n)
                    for turn_ in mine[BEFORE_SCORES[n]:BEFORE_MAXIMA[n]]:
                        if active(i, turn_[1]):
                            turn(i, parity, *turn_)
                    if n + M_AHEAD >= SLOTS:
                        if active(i, "front"):
                            scores_max(i, parity, n + M_AHEAD - SLOTS)
                    elif active(i, "attn"):
                        scores_max(i - 1, 1 - parity, n + M_AHEAD)
                    for turn_ in mine[BEFORE_MAXIMA[n]:]:
                        if active(i, turn_[1]):
                            turn(i, parity, *turn_)
                    if (n - C_LAG) % 2 == 0:
                        p, j = divmod((n - C_LAG) // 2, NB)
                        if p >= 0 and active(i, "attn"):
                            contexts(i - 1, 1 - parity, p, j)
                        if p < 0 and active(i, "mid"):
                            contexts(i - 2, parity, PAIRS - 1, j)

            each_iteration(pe, body, after_first=setup_rest, after_second=weights_ready)


_INS = ['x', 'L0_tok_kernel', 'L0_tok_bias', 'L0_tok_beta', 'L0_tok_moving_mean', 'L0_tok_moving_var',
        'L0_attn_Q', 'L0_attn_K', 'L0_attn_VO', 'L0_ffn_W1', 'L0_ffn_b1', 'L0_ffn_Wg', 'L0_ffn_bg',
        'L0_ffn_Wd', 'L0_ffn_bd', 'L1_attn_Wq', 'L1_attn_Wk', 'L1_attn_Wv', 'L1_attn_Wo',
        'L1_ffn_router_w1', 'L1_ffn_router_b1', 'L1_ffn_router_w2', 'L1_ffn_router_b2',
        'L1_ffn_expert_w1', 'L1_ffn_expert_b1', 'L1_ffn_expert_w2', 'L1_ffn_expert_b2',
        'L1_ffn_expert_w3', 'L1_ffn_expert_b3']


def kernel(**inputs):
    import numpy as _np
    import concourse.bacc as _bacc
    from concourse import mybir as _mybir
    from concourse.bass_utils import run_bass_kernel_spmd as _run

    nc = _bacc.Bacc("TRN2", target_bir_lowering=False, num_devices=1)
    arrays, args = {}, []
    for name in _INS:
        a = _np.ascontiguousarray(inputs[name])
        arrays[f"in_{name}"] = a
        args.append(nc.dram_tensor(f"in_{name}", a.shape, _mybir.dt.from_np(a.dtype), kind="ExternalInput").ap())
    args.append(nc.dram_tensor("out_0", (B, T, D), F32, kind="ExternalOutput").ap())
    tower(nc, *args)
    r = _run(nc, [arrays], core_ids=[0])
    return r.results[0]["out_0"]
```
